# Optimizing a Trainium2 kernel written in Bass

```python
import numpy as np
import jax
import jax.numpy as jnp

def _softmax(x, axis=-1):
    return jax.nn.softmax(x, axis=axis)
def _gelu(x):
    return jax.nn.gelu(x, approximate=True)
def _silu(x):
    return jax.nn.silu(x)
def _sigmoid(x):
    return jax.nn.sigmoid(x)
def _layernorm(x, axis=-1, eps=1e-5):
    m = jnp.mean(x, axis=axis, keepdims=True)
    v = jnp.var(x, axis=axis, keepdims=True)
    return (x - m) / jnp.sqrt(v + eps)
def _scatter_add(tgt, idx, src, axis=0):
    return tgt.at[idx].add(src)
def _segment_sum(src, seg, n):
    return jax.ops.segment_sum(src, seg, n)

kernel_name = 'mk_adj_resnorm_d2_adj_256_4917a7'

def setup_inputs(seed: int = 0):
    np.random.seed(seed)
    _w = jnp.asarray
    def _rec_inputs():
        import jax
        import jax.numpy as jnp
        _gk = jax.random.key(seed)
        x = -0.0002928 + 1 * jax.random.normal(jax.random.fold_in(_gk, 1), (8, 2048, 256), jnp.float32)
        _a = jax.random.bernoulli(jax.random.fold_in(_gk, 2), 0.00390625, (2048, 2048))
        _a = jnp.logical_or(_a, jnp.swapaxes(_a, -1, -2))
        _a = jnp.logical_or(_a, jnp.eye(2048, dtype=bool))
        adj = _a.astype(jnp.int32)
        return x, adj
    x, adj = _rec_inputs()
    def _L0_gnn_setup():
        import jax, jax.numpy as jnp
        import numpy as np
        ALPHA = 0.2
        NEG_INF = -1000000000000.0
        key = jax.random.key(seed)
        k1, k2, k3, k4, k5 = jax.random.split(key, 5)
        B, N, C_in, C_out = (8, 2048, 256, 256)
        inp = jax.random.normal(k1, (B, N, C_in), dtype=jnp.float32)
        adj = jax.random.randint(k2, (N, N), 0, 2, dtype=jnp.int32)
        limit = 1.414 * np.sqrt(6.0 / (C_in + C_out))
        W1 = jax.random.uniform(k3, (C_in, C_out), jnp.float32, -limit, limit)
        W2 = jax.random.uniform(k4, (C_in, C_out), jnp.float32, -limit, limit)
        W3 = jax.random.uniform(k5, (C_in, C_out), jnp.float32, -limit, limit)
        return {'inp': inp, 'adj': adj, 'W1': W1, 'W2': W2, 'W3': W3}
    _L0_gnn_all = _L0_gnn_setup()
    _L0_gnn_in = {k: v for k, v in _L0_gnn_all.items() if k in ('W1', 'W2', 'W3', )}
    del _L0_gnn_all

    def _L1_gnn_setup():
        import jax, jax.numpy as jnp
        import numpy as np
        IN_DIM = 256
        OUT_DIM = 64
        NUM_HEADS = 4
        ALPHA = 0.2
        NEG_INF = -9000000000000000.0
        key = jax.random.key(seed)
        k1, k2, k3, k4 = jax.random.split(key, 4)
        B, N = (4, 2048)
        h = jax.random.normal(k1, (B, N, IN_DIM), dtype=jnp.float32)
        adj = jax.random.randint(k2, (N, N), 0, 2, dtype=jnp.int32)
        W = jax.random.normal(k3, (IN_DIM, NUM_HEADS * OUT_DIM), dtype=jnp.float32) * (1.0 / np.sqrt(IN_DIM))
        a = jax.random.normal(k4, (2 * OUT_DIM,), dtype=jnp.float32) * (1.0 / np.sqrt(2 * OUT_DIM))
        return {'h': h, 'adj': adj, 'W': W, 'a': a}
    _L1_gnn_all = _L1_gnn_setup()
    _L1_gnn_in = {k: v for k, v in _L1_gnn_all.items() if k in ('W', 'a', )}
    del _L1_gnn_all

    return {
        "x": x,
        "adj": adj,
        "L0_gnn_W1": _L0_gnn_in["W1"],
        "L0_gnn_W2": _L0_gnn_in["W2"],
        "L0_gnn_W3": _L0_gnn_in["W3"],
        "L1_gnn_W": _L1_gnn_in["W"],
        "L1_gnn_a": _L1_gnn_in["a"],
    }

def reference(x, adj, L0_gnn_W1, L0_gnn_W2, L0_gnn_W3, L1_gnn_W, L1_gnn_a):
    import jax
    import jax.numpy as jnp
    def _L0_gnn_ref(inp, adj, W1, W2, W3):
        import jax, jax.numpy as jnp
        import numpy as np
        ALPHA = 0.2
        NEG_INF = -1000000000000.0
        h1 = jnp.einsum('bnc,cd->bnd', inp, W1)
        h2 = jnp.einsum('bnc,cd->bnd', inp, W2)
        h3 = jnp.einsum('bnc,cd->bnd', inp, W3)
        e = jnp.einsum('bnd,bmd->bnm', h1, h2)
        e = jax.nn.leaky_relu(e, ALPHA)
        e = jnp.where(adj[None, :, :] > 0, e, NEG_INF)
        attention = jax.nn.softmax(e, axis=-1)
        h_prime = jnp.einsum('bnm,bmd->bnd', attention, h3)
        return jax.nn.relu(h_prime)

    def _L1_gnn_ref(h, adj, W, a):
        import jax, jax.numpy as jnp
        import numpy as np
        IN_DIM = 256
        OUT_DIM = 64
        NUM_HEADS = 4
        ALPHA = 0.2
        NEG_INF = -9000000000000000.0
        B, N, _ = h.shape
        H, D = (NUM_HEADS, OUT_DIM)
        q = (h @ W).reshape(B, N, H, D)
        a_src, a_dst = (a[:D], a[D:])
        e_src = jnp.einsum('bnhd,d->bnh', q, a_src)
        e_dst = jnp.einsum('bnhd,d->bnh', q, a_dst)
        e = e_src[:, :, None, :] + e_dst[:, None, :, :]
        e = jnp.where(e >= 0, e, ALPHA * e)
        mask = (adj > 0)[None, :, :, None]
        e = jnp.where(mask, e, NEG_INF)
        attn = jax.nn.softmax(e, axis=2)
        h_prime = jnp.einsum('bijh,bjhd->bihd', attn, q)
        return jax.nn.elu(h_prime.reshape(B, N, H * D))

    x = _layernorm(x + _L0_gnn_ref(x, adj, L0_gnn_W1, L0_gnn_W2, L0_gnn_W3), axis=-1)
    x = _layernorm(x + _L1_gnn_ref(x, adj, L1_gnn_W, L1_gnn_a), axis=-1)
    return x


_drawn_inputs = setup_inputs


def setup_inputs(seed=0):
    import zlib

    import numpy as np

    out = dict(_drawn_inputs(seed))
    spreads = {}
    factors = {}
    for name, (base, spread) in spreads.items():
        noise = np.random.default_rng([zlib.crc32(name.encode()), seed]).standard_normal(out[name].shape)
        drawn = base * np.exp(spread * noise) if base else spread * noise
        out[name] = jnp.asarray(drawn.astype(out[name].dtype))
    for name, factor in factors.items():
        out[name] = (out[name] * factor).astype(out[name].dtype)
    return out
```

```python
from contextlib import ExitStack

import concourse.bass as bass
from concourse import mybir

P = 128
F32 = mybir.dt.float32
F32R = mybir.dt.float32r
F16 = mybir.dt.float16
BF16 = mybir.dt.bfloat16
U8 = mybir.dt.uint8
I32 = mybir.dt.int32
ALU = mybir.AluOpType
ACT = mybir.ActivationFunctionType
AX = mybir.AxisListType

ALPHA = 0.2
EPS = 1e-5
MASKED = -1e30
LN_1024 = 6.931471805599453
CH = 512
TB = CH // P
HUGE = 2.0 ** 100
Q_SCALE = 2048.0
DEN_SCALE = 1024.0


def dynamic(start, size):
    return bass.ds(start, size)


class Fresh:

    def __init__(self, engine, name, largest):
        self.engine, self.register, self.largest = engine, engine.alloc_register(name), largest

    def __call__(self, value):
        if isinstance(value, int):
            return value
        self.engine.reg_mov(self.register, value)
        return self.engine.snap(self.register, min_val=0, max_val=self.largest)


def build_setup(nc, st, W1, W2, W3):
    ident, w3, a_hi, a_lo = st.ident, st.w3, st.a_hi, st.a_lo
    with ExitStack() as ctx:
        w1 = ctx.enter_context(nc.sbuf_tensor("w1_rows", [P, 2, 256], F32))
        w2 = ctx.enter_context(nc.sbuf_tensor("w2_rows", [P, 2, 256], F32))
        w1T = ctx.enter_context(nc.sbuf_tensor("w1T", [P, 2, 256], F32))
        w2T = ctx.enter_context(nc.sbuf_tensor("w2T", [P, 2, 256], F32))
        turned = ctx.enter_context(nc.psum_tensor("w_turned", [P, 4, CH], F32))
        a_ps = ctx.enter_context(nc.psum_tensor("a_ps", [P, 2, CH], F32))
        w_loaded = ctx.enter_context(nc.semaphore("w_loaded"))
        ident_zero = ctx.enter_context(nc.semaphore("ident_zero"))
        ident_ready = ctx.enter_context(nc.semaphore("ident_ready"))
        w_turned = ctx.enter_context(nc.semaphore("w_turned_ready"))
        wT_ready = ctx.enter_context(nc.semaphore("wT_ready"))
        a_ready = ctx.enter_context(nc.semaphore("a_ready"))
        a_hi_ready = ctx.enter_context(nc.semaphore("a_hi_ready"))
        block = ctx.enter_context(nc.Block())

        @block.sync
        def _(sp):
            for dst, src in ((w1, W1), (w2, W2), (w3, W3)):
                sp.dma_start(dst[:], src.rearrange("(k p) d -> p k d", p=P)).then_inc(w_loaded, 16)
            sp.wait_ge(w_loaded, 48)

        @block.gpsimd
        def _(pool):
            nc.gpsimd.memset(ident[:], 0.0).then_inc(ident_zero, 1)
            nc.gpsimd.memset(st.minus_half[:], -0.5)
            pool.wait_ge(ident_zero, 1)
            nc.gpsimd.affine_select(out=ident[:], in_=ident[:], compare_op=ALU.not_equal, fill=1.0,
                                    base=0, pattern=[[-1, P]], channel_multiplier=1).then_inc(ident_ready, 1)

        @block.tensor
        def _(pe):
            pe.wait_ge(w_loaded, 48)
            pe.wait_ge(ident_ready, 1)
            for n, w in enumerate((w1, w2)):
                for dk in range(2):
                    for ck in range(2):
                        ins = nc.tensor.transpose(turned[:, 2 * n + dk, ck * P:(ck + 1) * P],
                                                  w[:, ck, dk * P:(dk + 1) * P], ident[:])
            ins.then_inc(w_turned, 1)
            pe.wait_ge(wT_ready, 4)
            for ck in range(2):
                for dk in range(2):
                    ins = nc.tensor.matmul(a_ps[:, ck, 0:256], w1T[:, dk, ck * P:(ck + 1) * P],
                                           w2T[:, dk, :], start=(dk == 0), stop=(dk == 1))
            ins.then_inc(a_ready, 1)

        @block.vector
        def _(dve):
            dve.wait_ge(w_turned, 1)
            for n, wT in enumerate((w1T, w2T)):
                for dk in range(2):
                    nc.vector.tensor_copy(wT[:, dk, :], turned[:, 2 * n + dk, 0:256]).then_inc(wT_ready, 1)
            dve.wait_ge(a_ready, 1)
            for ck in range(2):
                nc.vector.tensor_copy(a_hi[:, ck, :], a_ps[:, ck, 0:256]).then_inc(a_hi_ready, 1)
            dve.wait_ge(a_hi_ready, 2)
            for ck in range(2):
                nc.vector.tensor_tensor(a_lo[:, ck, :], a_ps[:, ck, 0:256],
                                        a_hi[:, ck, :].bitcast(F32), ALU.subtract)
            nc.vector.memset(st.h3_hi[:, :, 256:257], 1.0)


def build_dense(nc, st, x, adj, x1):
    B, N, C = x.shape
    NB = N // CH
    NT = N // P
    BLOCKS = B * NB
    SLOTS = 2 * NB
    KC = C // P
    ALL = B * NT
    x_rows = x.rearrange("b n c -> (b n) c")
    x1_rows = x1.rearrange("b n c -> (b n) c")
    ident, w3, a_hi, a_lo, notadj, h3_hi = st.ident, st.w3, st.a_hi, st.a_lo, st.notadj, st.h3_hi
    PREP_AT = {0: (0, 1), 1: (2,), 2: (3,), 3: ()}
    Y_AT = {0: 0, 1: 1}
    Y_SPLIT_AT = 2
    TURN_AT = {NB // 2 - 1: 0, NB // 2: 1}

    with ExitStack() as ctx:
        def sb(name, shape, dt):
            return ctx.enter_context(nc.sbuf_tensor(name, shape, dt))

        def ps(name, shape, dt=F32):
            return ctx.enter_context(nc.psum_tensor(name, shape, dt))

        def sem(name):
            return ctx.enter_context(nc.semaphore(name))

        xT_hi = sb("xT_hi", [P, SLOTS, KC, CH], F32R)
        xT_lo = sb("xT_lo", [P, SLOTS, KC, CH], F32R)
        h3_lo = sb("h3_lo", [P, 2 * NT, C], F16)
        y_raw = sb("y_raw", [P, KC, CH], F32)
        y_hi = sb("y_hi", [P, KC, CH], F32R)
        y_lo = sb("y_lo", [P, KC, CH], F32R)
        relu_e = sb("relu_e", [P, N], F32)
        probs = sb("probs", [P, 2, N], F32)
        pT_hi = sb("pT_hi", [P, TB, CH], F16)
        pT_lo = sb("pT_lo", [P, TB, CH], F16)
        x_in = sb("x_in", [P, TB, C], F32)
        x_res = sb("x_res", [P, TB, C], F32)
        xT_raw = sb("xT_raw", [P, 2, KC, P], F32)
        gat = sb("gat", [P, 2, C], F32)
        summed = sb("summed", [P, 2, C], F32)
        x1_out = sb("x1_out", [P, TB, C], F32)
        bankmax = sb("bankmax", [P, 2, NB], F32)
        rowmax = sb("rowmax", [P, 2], F32)
        shift = sb("shift", [P, 2], F32)
        rden = sb("rden", [P, 2], F32)
        stats = sb("stats", [P, 2, 6], F32)
        meanvar = sb("meanvar", [P, 2, 2], F32)
        vareps = sb("vareps", [P, 2], F32)
        rstd = sb("rstd", [P, 2], F32)
        adj_in = sb("adj_in", [P, N], I32)

        e_ps = ps("e_ps", [P, NB, CH])
        pT_ps = ps("pT_ps", [P, 2, CH])
        out_ps = ps("out_ps", [P, CH])
        misc_ps = ps("misc_ps", [P, CH])

        x_in_full = [sem(f"x_in_full{k}") for k in range(TB)]
        x_res_full = [sem(f"x_res_full{k}") for k in range(TB)]
        x1_stored = [sem(f"x1_stored{k}") for k in range(TB)]
        adj_full = sem("adj_full")
        mask_made = sem("mask_made")
        xT_turned = sem("xT_turned")
        xT_raw_full = sem("xT_raw_full")
        xT_hi_full = sem("xT_hi_full")
        xT_lo_full = sem("xT_lo_full")
        h3_made = sem("h3_made")
        h3_hi_full = sem("h3_hi_full")
        h3_lo_full = sem("h3_lo_full")
        y_made = sem("y_made")
        y_raw_full = sem("y_raw_full")
        y_hi_full = sem("y_hi_full")
        y_lo_full = sem("y_lo_full")
        e_made = sem("e_made")
        relu_e_full = sem("relu_e_full")
        edges_full = sem("edges_full")
        masked_full = sem("masked_full")
        rowmax_full = sem("rowmax_full")
        shift_full = sem("shift_full")
        probs_full = sem("probs_full")
        pT_turned = sem("pT_turned")
        pT_hi_full = sem("pT_hi_full")
        pT_lo_full = sem("pT_lo_full")
        pv_made = sem("pv_made")
        rden_full = sem("rden_full")
        gat_full = sem("gat_full")
        summed_full = sem("summed_full")
        stats_full = sem("stats_full")
        meanvar_full = sem("meanvar_full")
        vareps_full = sem("vareps_full")
        rstd_full = sem("rstd_full")
        x1_full = sem("x1_full")

        block = ctx.enter_context(nc.Block())

        runs = [(1, NB - 1, True, True), (NB - 1, BLOCKS - NB, False, True),
                (BLOCKS - NB, BLOCKS - 1, False, False)]

        def over_blocks(engine, step):
            step(0, True, True, True)
            for first, end, masks, preps in runs:
                if first < end:
                    with engine.Fori(first, end) as it:
                        step(it, masks, preps, True)
            step(BLOCKS - 1, False, False, False)

        def preps_before(it, preps):
            return NT + TB * it if preps else ALL

        def prep_slot(it):
            return (it + NB) % SLOTS

        def batch_slot(it):
            return (it // NB) % 2 * NB

        @block.sync
        def _(sp):
            def load_adj(tile, n):
                if not (isinstance(n, int) and n == 0):
                    sp.wait_ge(mask_made, n)
                sp.dma_start(adj_in[:], adj[dynamic(tile * P, P), :]).then_inc(adj_full, 16)

            def load_x(row_tile, k, n):
                if not (isinstance(n, int) and n <= 0):
                    sp.wait_ge(xT_turned, n)
                sp.dma_start(x_in[:, k, :], x_rows[dynamic(row_tile * P, P), :]).then_inc(x_in_full[k], 16)

            for k in range(TB):
                load_x(k, k, 0)
            load_adj(0, 0)
            with sp.Fori(1, NB) as j:
                for k in range(TB):
                    load_x(TB * j + k, k, TB * j - TB + k + 1)
            for k in range(1, TB):
                load_adj(k, k)

            def step(it, masks, preps, more):
                for k in range(TB):
                    if not (isinstance(it, int) and it == 0):
                        sp.wait_ge(summed_full, TB * it - TB + k + 1)
                    sp.dma_start(x_res[:, k, :], x_rows[dynamic((TB * it + k) * P, P), :]).then_inc(x_res_full[k], 16)
                for k in range(TB):
                    if preps:
                        load_x(NT + TB * it + k, k, NT + TB * it - TB + k + 1)
                for k in range(TB):
                    if masks:
                        load_adj(TB * it + TB + k, TB * it + TB + k)
                    sp.wait_ge(x1_full, TB * it + k + 1)
                    sp.dma_start(x1_rows[dynamic((TB * it + k) * P, P), :], x1_out[:, k, :]).then_inc(x1_stored[k], 16)

            over_blocks(sp, step)
            for k in range(TB):
                sp.wait_ge(x1_stored[k], 16 * BLOCKS)

        @block.tensor
        def _(pe):
            fresh_slot = Fresh(pe, "fresh_slot", NB)

            def turn_x(n, k, round_):
                pe.wait_ge(x_in_full[k], 16 * round_)
                if not (isinstance(n, int) and n == 0):
                    pe.wait_ge(h3_lo_full, n)
                for c in range(KC):
                    ins = nc.tensor.transpose(misc_ps[:, c * P:(c + 1) * P],
                                              x_in[:, k, c * P:(c + 1) * P], ident[:])
                ins.then_inc(xT_turned, 1)

            def make_h3(n, k):
                pe.wait_ge(xT_raw_full, n + 1)
                for c in range(KC):
                    ins = nc.tensor.matmul(misc_ps[:, 0:C], xT_raw[:, k % 2, c, :], w3[:, c, :],
                                           start=(c == 0), stop=(c == KC - 1))
                ins.then_inc(h3_made, 1)

            def make_y(half, slot):
                passes = [(a, xt) for a, xt in ((a_hi, xT_hi), (a_hi, xT_lo), (a_lo, xT_hi))]
                for c in range(KC):
                    for m, (a, xt) in enumerate(passes):
                        ins = nc.tensor.matmul(misc_ps[:], a[:, c, half * P:(half + 1) * P],
                                               xt[:, slot, c, :] if isinstance(slot, int)
                                               else xt[:, dynamic(slot, 1), c, :],
                                               start=(c == 0 and m == 0),
                                               stop=(c == KC - 1 and m == len(passes) - 1))
                ins.then_inc(y_made, 1)

            def make_e(tile, k, base, between=None):
                base = fresh_slot(base)
                passes = ((y_hi, xT_hi), (y_hi, xT_lo), (y_lo, xT_hi))
                for bank in range(NB):
                    if not (isinstance(tile, int) and tile == 0):
                        pe.wait_ge(masked_full, NB * tile - NB + bank + 1)
                    for c in range(KC):
                        for m, (y, xt) in enumerate(passes):
                            ins = nc.tensor.matmul(e_ps[:, bank, :], y[:, c, k * P:(k + 1) * P],
                                                   xt[:, dynamic(base + bank, 1), c, :],
                                                   start=(c == 0 and m == 0),
                                                   stop=(c == KC - 1 and m == len(passes) - 1))
                    ins.then_inc(e_made, 1)
                    if between and bank in TURN_AT:
                        between(TURN_AT[bank])

            def turn_p(tile, k, c):
                if c == 0:
                    pe.wait_ge(probs_full, tile + 1)
                n = NB * tile + c - 1
                if not (isinstance(n, int) and n <= 0):
                    pe.wait_ge(pT_lo_full, n)
                for m in range(TB):
                    ins = nc.tensor.transpose(pT_ps[:, c % 2, m * P:(m + 1) * P],
                                              probs[:, k % 2, (TB * c + m) * P:(TB * c + m + 1) * P],
                                              ident[:])
                ins.then_inc(pT_turned, 1)

            def make_pv(tile, k, c, base):
                pe.wait_ge(pT_lo_full, NB * tile + c + 1)
                base = fresh_slot(base)
                if c == 0 and not (isinstance(tile, int) and tile == 0):
                    pe.wait_ge(gat_full, tile)
                for m in range(TB):
                    j = base * TB + TB * c + m
                    hi, lo = h3_hi[:, dynamic(j, 1), :], h3_lo[:, dynamic(j, 1), :]
                    first = c == 0 and m == 0
                    last = c == NB - 1 and m == TB - 1
                    w_hi = pT_hi[:, c, m * P:(m + 1) * P]
                    w_lo = pT_lo[:, c, m * P:(m + 1) * P]
                    nc.tensor.matmul(out_ps[:, 0:C + 1], w_hi, hi, start=first, stop=False)
                    nc.tensor.matmul(out_ps[:, 0:C], w_hi, lo, start=False, stop=False)
                    ins = nc.tensor.matmul(out_ps[:, 0:C + 1], w_lo, hi, start=False, stop=last)
                ins.then_inc(pv_made, 1)

            for k in range(TB):
                turn_x(k, k, 1)
                make_h3(k, k)
            with pe.Fori(1, NB) as j:
                for k in range(TB):
                    turn_x(TB * j + k, k, j + 1)
                    make_h3(TB * j + k, k)
            pe.wait_ge(h3_lo_full, NT)
            pe.wait_ge(xT_lo_full, NT)
            make_y(0, 0)
            pe.wait_ge(y_raw_full, 1)
            make_y(1, 0)
            pe.wait_ge(y_lo_full, 1)
            make_e(0, 0, 0)

            def step(it, masks, preps, more):
                n = preps_before(it, preps)
                tile = TB * it
                base = batch_slot(it)
                for k in range(TB):
                    todo = list(PREP_AT[k]) if preps else []
                    made = sum(len(PREP_AT[i]) for i in range(k)) if preps else 0
                    if todo:
                        pe.wait_ge(y_raw_full, 2 * it + 2 + sum(i < k for i in Y_AT))
                        turn_x(n + made, todo[0], NB + it + 1)

                    def first_turns(c, tile=tile, k=k):
                        turn_p(tile + k, k, c)

                    if k < TB - 1:
                        make_e(tile + k + 1, k + 1, base, first_turns)
                    elif more:
                        pe.wait_ge(y_lo_full, it + 2)
                        pe.wait_ge(xT_lo_full, n + (TB if preps else 0))
                        make_e(tile + TB, 0, batch_slot(it + 1), first_turns)
                    else:
                        first_turns(0)
                        first_turns(1)
                    if todo:
                        make_h3(n + made, todo[0])
                    for c in range(NB):
                        make_pv(tile + k, k, c, base)
                        if c + 2 < NB:
                            turn_p(tile + k, k, c + 2)
                        if c == 0 and len(todo) > 1:
                            turn_x(n + made + 1, todo[1], NB + it + 1)
                        if c == 1 % NB and len(todo) > 1:
                            make_h3(n + made + 1, todo[1])
                        if c == NB - 1 and more and k in Y_AT:
                            done = made + len(todo)
                            pe.wait_ge(h3_lo_full, n + done)
                            pe.wait_ge(xT_lo_full, n)
                            pe.wait_ge(y_raw_full, 2 * it + 2 + sum(i < k for i in Y_AT))
                            make_y(Y_AT[k], (it + 1) % SLOTS)

            over_blocks(pe, step)

        @block.scalar
        def _(act):
            def copy_xT(n, k):
                act.wait_ge(xT_turned, n + 1)
                if not (isinstance(n, int) and n < 2):
                    act.wait_ge(h3_made, n - 1)
                    act.wait_ge(xT_lo_full, n - 1)
                nc.scalar.activation(xT_raw[:, k % 2, :, :].rearrange("p c n -> p (c n)"), misc_ps[:, 0:C],
                                     ACT.Copy).then_inc(xT_raw_full, 1)

            def copy_h3(n, k, slot, pv):
                act.wait_ge(h3_made, n + 1)
                if pv is not None:
                    act.wait_ge(pv_made, pv)
                nc.scalar.activation(h3_hi[:, dynamic(slot * TB + k, 1), 0:C], misc_ps[:, 0:C],
                                     ACT.Copy).then_inc(h3_hi_full, 1)

            def copy_y(half, n):
                act.wait_ge(y_made, n + 1)
                if not (isinstance(n, int) and n < 2):
                    act.wait_ge(y_lo_full, (n - half) // 2 if isinstance(n, int) else n)
                nc.scalar.activation(y_raw[:, half, :], misc_ps[:], ACT.Copy).then_inc(y_raw_full, 1)

            def split_y(blocks):
                act.wait_ge(y_raw_full, 2 * blocks + 2)
                if not (isinstance(blocks, int) and blocks == 0):
                    act.wait_ge(e_made, NB * TB * blocks)
                nc.scalar.activation(y_hi[:], y_raw[:], ACT.Copy).then_inc(y_hi_full, 1)

            def positive_part(tile, between=None):
                for bank in range(NB):
                    act.wait_ge(e_made, NB * tile + bank + 1)
                    if not (isinstance(tile, int) and tile == 0):
                        act.wait_ge(masked_full, NB * tile - NB + bank + 1)
                    nc.scalar.activation(relu_e[:, bank * CH:(bank + 1) * CH], e_ps[:, bank, :], ACT.Relu,
                                         scale=1 / ALPHA - 1).then_inc(relu_e_full, 1)
                    if between and bank in TURN_AT:
                        between(TURN_AT[bank])

            def exponentials(tile, k):
                act.wait_ge(shift_full, tile + 1)
                nc.scalar.activation(probs[:, k % 2, :], probs[:, k % 2, :], ACT.Exp,
                                     bias=shift[:, k % 2:k % 2 + 1]).then_inc(probs_full, 1)

            def copy_pT(tile, c):
                act.wait_ge(pT_turned, NB * tile + c + 1)
                n = NB * tile + c - NB + 1
                if not (isinstance(n, int) and n <= 0):
                    act.wait_ge(pv_made, n)
                nc.scalar.activation(pT_hi[:, c, :], pT_ps[:, c % 2, :], ACT.Copy).then_inc(pT_hi_full, 1)

            def relu(tile, k):
                act.wait_ge(rden_full, tile + 1)
                if not (isinstance(tile, int) and tile < 2):
                    act.wait_ge(summed_full, tile - 1)
                nc.scalar.activation(gat[:, k % 2, :], out_ps[:, 0:C], ACT.Relu,
                                     scale=rden[:, k % 2:k % 2 + 1]).then_inc(gat_full, 1)

            for k in range(TB):
                copy_xT(k, k)
                copy_h3(k, k, 0, None)
            with act.Fori(1, NB) as j:
                for k in range(TB):
                    copy_xT(TB * j + k, k)
                    copy_h3(TB * j + k, k, j, None)
            copy_y(0, 0)
            copy_y(1, 1)
            split_y(0)
            positive_part(0)
            exponentials(0, 0)

            def step(it, masks, preps, more):
                n = preps_before(it, preps)
                tile = TB * it
                for k in range(TB):
                    todo = list(PREP_AT[k]) if preps else []
                    made = sum(len(PREP_AT[i]) for i in range(k)) if preps else 0
                    if todo:
                        copy_xT(n + made, todo[0])

                    def first_copies(c, tile=tile, k=k):
                        copy_pT(tile + k, c)

                    if k < TB - 1 or more:
                        positive_part(tile + k + 1, first_copies)
                    else:
                        first_copies(0)
                        first_copies(1)
                    if k == Y_SPLIT_AT and more:
                        split_y(it + 1)
                    if todo:
                        copy_h3(n + made, todo[0], prep_slot(it), NB * tile)
                    for c in range(2, NB):
                        copy_pT(tile + k, c)
                        if c == 2 and len(todo) > 1:
                            copy_xT(n + made + 1, todo[1])
                    if NB == 2 and len(todo) > 1:
                        copy_xT(n + made + 1, todo[1])
                    if len(todo) > 1:
                        copy_h3(n + made + 1, todo[1], prep_slot(it), NB * tile)
                    if k < TB - 1 or more:
                        exponentials(tile + k + 1, k + 1)
                    if more and k in Y_AT:
                        act.wait_ge(y_made, 2 * it + 3 + Y_AT[k])
                        if Y_AT[k] == 0:
                            act.wait_ge(y_lo_full, it + 1)
                        nc.scalar.activation(y_raw[:, Y_AT[k], :], misc_ps[:], ACT.Copy).then_inc(y_raw_full, 1)
                    relu(tile + k, k)

            over_blocks(act, step)

        @block.vector
        def _(dve):
            def make_mask(n):
                dve.wait_ge(adj_full, 16 * (n + 1))
                dst = notadj[:, n, :] if isinstance(n, int) else notadj[:, dynamic(n, 1), :]
                nc.vector.tensor_scalar(dst, adj_in[:], 0.0, None, ALU.is_le).then_inc(mask_made, 1)

            def split_xT(n, k, slot, scores):
                dve.wait_ge(xT_raw_full, n + 1)
                if scores is not None:
                    dve.wait_ge(e_made, scores)
                raw = xT_raw[:, k % 2, :, :]
                hi = xT_hi[:, dynamic(slot, 1), :, k * P:(k + 1) * P].rearrange("p o c n -> p (o c) n")
                lo = xT_lo[:, dynamic(slot, 1), :, k * P:(k + 1) * P].rearrange("p o c n -> p (o c) n")
                nc.vector.tensor_copy(hi, raw).then_inc(xT_hi_full, 1)
                dve.wait_ge(xT_hi_full, n + 1)
                nc.vector.tensor_tensor(lo, raw, hi.bitcast(F32), ALU.subtract).then_inc(xT_lo_full, 1)

            def split_h3(n, k, slot):
                dve.wait_ge(h3_hi_full, n + 1)
                j = slot * TB + k
                nc.vector.tensor_tensor(h3_lo[:, dynamic(j, 1), :].rearrange("p o c -> p (o c)"), misc_ps[:, 0:C],
                                        h3_hi[:, dynamic(j, 1), 0:C].rearrange("p o c -> p (o c)"),
                                        ALU.subtract).then_inc(h3_lo_full, 1)

            def split_y(blocks):
                dve.wait_ge(y_hi_full, blocks + 1)
                nc.vector.tensor_tensor(y_lo[:], y_raw[:], y_hi[:].bitcast(F32), ALU.subtract).then_inc(y_lo_full, 1)

            def mask(tile, k, row_tile, between=None):
                if not (isinstance(tile, int) and tile < 2):
                    dve.wait_ge(pT_turned, NB * tile - NB)
                for bank in range(NB):
                    cols = slice(bank * CH, (bank + 1) * CH)
                    dve.wait_ge(relu_e_full, NB * tile + bank + 1)
                    nc.vector.scalar_tensor_tensor(
                        out=relu_e[:, cols], in0=notadj[:, dynamic(row_tile, 1), cols].rearrange("p o n -> p (o n)"),
                        scalar=MASKED, in1=relu_e[:, cols], op0=ALU.mult, op1=ALU.add).then_inc(edges_full, 1)
                    dve.wait_ge(edges_full, 1)
                    dve.wait_ge(edges_full, NB * tile + bank + 1)
                    nc.vector.tensor_tensor_reduce(
                        out=probs[:, k % 2, cols], in0=e_ps[:, bank, :], in1=relu_e[:, cols], scale=ALPHA,
                        scalar=-3e38, op0=ALU.add, op1=ALU.max,
                        accum_out=bankmax[:, k % 2, bank:bank + 1]).then_inc(masked_full, 1)
                    if between and bank in TURN_AT:
                        between(TURN_AT[bank])

            def maximum(tile, k):
                dve.wait_ge(masked_full, NB * tile + NB)
                nc.vector.tensor_reduce(rowmax[:, k % 2:k % 2 + 1], bankmax[:, k % 2, :], AX.X,
                                        ALU.max).then_inc(rowmax_full, 1)
                dve.wait_ge(rowmax_full, tile + 1)
                if not (isinstance(tile, int) and tile < 2):
                    dve.wait_ge(probs_full, tile - 1)
                nc.vector.tensor_scalar(shift[:, k % 2:k % 2 + 1], rowmax[:, k % 2:k % 2 + 1], -1.0, LN_1024,
                                        ALU.mult, ALU.add).then_inc(shift_full, 1)

            def split_pT(tile, c):
                dve.wait_ge(pT_hi_full, NB * tile + c + 1)
                nc.vector.tensor_tensor(pT_lo[:, c, :], pT_ps[:, c % 2, :], pT_hi[:, c, :],
                                        ALU.subtract).then_inc(pT_lo_full, 1)

            def invert(tile, k):
                dve.wait_ge(pv_made, NB * tile + NB)
                if not (isinstance(tile, int) and tile < 2):
                    dve.wait_ge(gat_full, tile - 1)
                nc.vector.reciprocal(rden[:, k % 2:k % 2 + 1], out_ps[:, C:C + 1]).then_inc(rden_full, 1)

            def residual(tile, k, it):
                s = k % 2
                dve.wait_ge(gat_full, tile + 1)
                dve.wait_ge(x_res_full[k], 16 * it + 16)
                nc.vector.tensor_tensor(summed[:, s, :], gat[:, s, :], x_res[:, k, :],
                                        ALU.add).then_inc(summed_full, 1)
                dve.wait_ge(summed_full, tile + 1)
                nc.vector.bn_stats(stats[:, s, :], summed[:, s, :]).then_inc(stats_full, 1)
                dve.wait_ge(stats_full, 1)
                dve.wait_ge(stats_full, tile + 1)
                nc.vector.bn_aggr(meanvar[:, s, :], stats[:, s, :]).then_inc(meanvar_full, 1)
                dve.wait_ge(meanvar_full, tile + 1)
                nc.vector.tensor_scalar(vareps[:, s:s + 1], meanvar[:, s, 1:2], EPS, None,
                                        ALU.add).then_inc(vareps_full, 1)

            def normalise(tile, k, it):
                s = k % 2
                dve.wait_ge(rstd_full, tile + 1)
                if not (isinstance(it, int) and it == 0):
                    dve.wait_ge(x1_stored[k], 16 * it)
                nc.vector.tensor_scalar(x1_out[:, k, :], summed[:, s, :], meanvar[:, s, 0:1], rstd[:, s:s + 1],
                                        ALU.subtract, ALU.mult).then_inc(x1_full, 1)

            for k in range(TB):
                split_xT(k, k, 0, None)
                split_h3(k, k, 0)
            with dve.Fori(1, NB) as j:
                for k in range(TB):
                    split_xT(TB * j + k, k, j, None)
                    split_h3(TB * j + k, k, j)
            for k in range(TB):
                make_mask(k)
            split_y(0)
            mask(0, 0, 0)
            maximum(0, 0)

            def step(it, masks, preps, more):
                n = preps_before(it, preps)
                tile = TB * it
                for k in range(TB):
                    todo = list(PREP_AT[k]) if preps else []
                    made = sum(len(PREP_AT[i]) for i in range(k)) if preps else 0
                    if k > 0:
                        normalise(tile + k - 1, k - 1, it)
                    if todo:
                        split_xT(n + made, todo[0], prep_slot(it), NB * tile)

                    def first_splits(c, tile=tile, k=k):
                        split_pT(tile + k, c)

                    if k < TB - 1:
                        mask(tile + k + 1, k + 1, (it % NB) * TB + k + 1, first_splits)
                    elif more:
                        mask(tile + TB, 0, (it + 1) % NB * TB, first_splits)
                    else:
                        first_splits(0)
                        first_splits(1)
                    if k < TB - 1 or more:
                        maximum(tile + k + 1, k + 1)
                    if k == Y_SPLIT_AT and more:
                        split_y(it + 1)
                    if todo:
                        split_h3(n + made, todo[0], prep_slot(it))
                    for c in range(2, NB):
                        split_pT(tile + k, c)
                        if c == 2 and len(todo) > 1:
                            split_xT(n + made + 1, todo[1], prep_slot(it), NB * tile)
                    if NB == 2 and len(todo) > 1:
                        split_xT(n + made + 1, todo[1], prep_slot(it), NB * tile)
                    if len(todo) > 1:
                        split_h3(n + made + 1, todo[1], prep_slot(it))
                    if masks:
                        make_mask(TB * it + TB + k)
                    invert(tile + k, k)
                    residual(tile + k, k, it)
                normalise(tile + TB - 1, TB - 1, it)

            over_blocks(dve, step)

        @block.gpsimd
        def _(pool):
            with pool.Fori(0, BLOCKS) as it:
                for k in range(TB):
                    s = k % 2
                    pool.wait_ge(vareps_full, TB * it + k + 1)
                    nc.gpsimd.tensor_tensor(rstd[:, s:s + 1], vareps[:, s:s + 1], st.minus_half[:, 0:1],
                                            ALU.pow).then_inc(rstd_full, 1)


def build_edges(nc, st, W, a):
    NT, N = st.notadj.shape[1], st.notadj.shape[2]
    C = W.shape[0]
    KC = C // P
    D = a.shape[0] // 2
    H = C // D
    ident, notadj, adjT, edgeless, w_ext = st.ident, st.notadj, st.adjT, st.edgeless, st.w_ext
    with ExitStack() as ctx:
        def sb(name, shape, dt):
            return ctx.enter_context(nc.sbuf_tensor(name, shape, dt))

        def sem(name):
            return ctx.enter_context(nc.semaphore(name))

        edge_rows = sb("edge_rows", [P, 2, N], BF16)
        ident16 = sb("ident16", [P, P], BF16)
        ones16 = sb("ones16", [P, 2], BF16)
        a_rows = sb("a_rows", [P, 2, D], F32)
        w_in = sb("w_in", [P, KC, C], F32)
        products = sb("products", [P, KC, 3, C], F32)
        squares = sb("squares", [P, KC], F32)
        square_sum = sb("square_sum", [P, 3], F32)
        scale = sb("scale", [P, 2], F32)
        turned = ctx.enter_context(nc.psum_tensor("edges_turned_ps", [P, NT, P], BF16))
        degree = ctx.enter_context(nc.psum_tensor("degree", [P, N], F32))

        small_loaded = sem("small_loaded")
        rows_full = sem("rows_full")
        rows_turned = sem("rows_turned")
        rows_copied = sem("rows_copied")
        ident16_full = sem("ident16_full")
        degree_made = sem("degree_made")
        chain = sem("w_steps")
        squares_full = sem("squares_full")
        reduced = sem("reduced")
        scale_full = sem("scale_full")
        squares_ready = sem("squares_ready")
        scaled = sem("scaled")
        block = ctx.enter_context(nc.Block())

        @block.sync
        def _(sp):
            sp.dma_start(w_in[:], W.rearrange("(k p) d -> p k d", p=P)).then_inc(small_loaded, 16)
            sp.dma_start(a_rows[:].rearrange("p s d -> p (s d)"), a.partition_broadcast(P)).then_inc(small_loaded, 16)
            sp.wait_ge(small_loaded, 32)

        @block.gpsimd
        def _(pool):
            nc.gpsimd.memset(st.mean_ones[:], 1.0 / N)
            nc.gpsimd.memset(st.den_scale[:], DEN_SCALE)
            pool.wait_ge(squares_full, 1)
            nc.gpsimd.partition_all_reduce(square_sum[:, 1:2], square_sum[:, 0:1], P,
                                           bass.bass_isa.ReduceOp.add).then_inc(reduced, 1)
            pool.wait_ge(reduced, 1)
            nc.gpsimd.tensor_tensor(scale[:, 0:1], square_sum[:, 1:2], st.minus_half[:], ALU.pow).then_inc(scale_full, 1)

        @block.tensor
        def _(pe):
            pe.wait_ge(ident16_full, 1)
            with pe.Fori(0, NT // 2) as pair:
                for k in range(2):
                    pe.wait_ge(rows_full, 2 * pair + k + 1)
                    pe.wait_ge(rows_copied, 2 * pair + k)
                    for j in range(NT):
                        ins = nc.tensor.transpose(turned[:, j, :], edge_rows[:, k, j * P:(j + 1) * P], ident16[:])
                    ins.then_inc(rows_turned, 1)
            pe.wait_ge(rows_copied, NT)
            for j in range(NT):
                for c in range(N // CH):
                    ins = nc.tensor.matmul(degree[0:1, c * CH:(c + 1) * CH], ones16[:, 0:1],
                                           adjT[:, j, c * CH:(c + 1) * CH], start=(j == 0), stop=(j == NT - 1))
            ins.then_inc(degree_made, 1)

        @block.scalar
        def _(act):
            with act.Fori(0, NT) as t:
                act.wait_ge(rows_turned, t + 1)
                nc.scalar.activation(adjT[:, :, dynamic(t * P, P)], turned[:], ACT.Copy).then_inc(rows_copied, 1)

        @block.vector
        def _(dve):
            nc.vector.memset(ones16[:], 1.0)
            nc.vector.memset(st.mean_lo[:], 0.0)
            nc.vector.memset(st.mean_hi[:], DEN_SCALE)
            nc.vector.tensor_copy(ident16[:], ident[:]).then_inc(ident16_full, 1)
            with dve.Fori(0, NT // 2) as pair:
                for k in range(2):
                    dve.wait_ge(rows_turned, 2 * pair)
                    nc.vector.tensor_scalar(edge_rows[:, k, :],
                                            notadj[:, dynamic(2 * pair + k, 1), :].rearrange("p o n -> p (o n)"),
                                            -1.0, 1.0, ALU.mult, ALU.add).then_inc(rows_full, 1)
            dve.wait_ge(small_loaded, 32)
            for c in range(KC):
                for s in range(2):
                    for h in range(H):
                        cols = slice(h * D, (h + 1) * D)
                        nc.vector.tensor_tensor_reduce(
                            out=products[:, c, s, cols], in0=w_in[:, c, cols], in1=a_rows[:, s, :], scale=1.0,
                            scalar=0.0, op0=ALU.mult, op1=ALU.add,
                            accum_out=w_ext[:, c, C + s * H + h:C + s * H + h + 1]).then_inc(chain, 1)
                dve.wait_ge(chain, (c + 1) * 2 * H)
                nc.vector.tensor_tensor_reduce(
                    out=products[:, c, 2, :], in0=w_in[:, c, :], in1=w_in[:, c, :], scale=1.0,
                    scalar=1e-30, op0=ALU.mult, op1=ALU.add, accum_out=squares[:, c:c + 1]).then_inc(squares_ready, 1)
            dve.wait_ge(squares_ready, KC)
            nc.vector.tensor_reduce(square_sum[:, 0:1], squares[:], AX.X, ALU.add).then_inc(squares_full, 1)
            dve.wait_ge(scale_full, 1)
            nc.vector.tensor_scalar(scale[:, 1:2], scale[:, 0:1], Q_SCALE, None, ALU.mult).then_inc(scaled, 1)
            dve.wait_ge(scaled, 1)
            for c in range(KC):
                nc.vector.tensor_scalar(w_ext[:, c, 0:C], w_in[:, c, :], scale[:, 1:2], None, ALU.mult)
            nc.vector.reciprocal(square_sum[:, 2:3], scale[:, 1:2]).then_inc(scaled, 1)
            dve.wait_ge(scaled, 2)
            nc.vector.tensor_scalar(st.unscale[:], square_sum[:, 2:3], DEN_SCALE, None, ALU.mult)
            dve.wait_ge(degree_made, 1)
            nc.vector.tensor_scalar(edgeless[:], degree[0:1, :], 0.0, None, ALU.is_equal)


def build_heads(nc, st, x1, s_rows, out):
    B, N, C = x1.shape
    NT = N // P
    KC = C // P
    D = 64
    H = C // D
    E = D + 1
    Q = C + 2 * H
    GROUPS = CH // (2 * E)
    BANKS = -(-NT // GROUPS)
    DEPTH = 4
    RUNS = NT // DEPTH
    x1_rows = x1.rearrange("b n c -> (b n) c")
    out_rows = out.rearrange("b n c -> (b n) c")
    ident, adjT, edgeless, w_ext = st.ident, st.adjT, st.edgeless, st.w_ext
    mean_hi, mean_lo = st.mean_hi, st.mean_lo

    with ExitStack() as ctx:
        def sb(name, shape, dt):
            return ctx.enter_context(nc.sbuf_tensor(name, shape, dt))

        def sem(name):
            return ctx.enter_context(nc.semaphore(name))

        def ps(name, shape):
            return ctx.enter_context(nc.psum_tensor(name, shape, F32))

        x_in = sb("hx_in", [P, 4, C], F32)
        xT = sb("hxT", [P, 2, KC, P], F32)
        q = sb("q", [P, NT, Q], F32)
        s_cols = sb("s_cols", [P, H, NT], F32)
        s_turned_sb = sb("s_turned_sb", [H * NT, P], F32)
        s_all = sb("s_all", [P, 2, N], F32)
        d_max = sb("d_max", [P, 2, H], F32)
        d_less = sb("d_less", [P, NT, H], F32)
        s_more = sb("s_more", [P, NT, H], F32)
        d_huge = sb("d_huge", [P, NT, H], F32)
        low_factor = sb("low_factor", [P, NT, H], F32)
        up_factor = sb("up_factor", [P, NT, H], F32)
        row_factor = sb("row_factor", [P, NT, H], F32)
        values = sb("values", [P, 2, NT, E], F32)
        up_hi = sb("up_hi", [P, 2, NT, E], F16)
        up_lo = sb("up_lo", [P, 2, NT, E], F16)
        low_hi = sb("low_hi", [P, 2, NT, E], F16)
        low_lo = sb("low_lo", [P, 2, NT, E], F16)
        upper = sb("upper", [P, DEPTH, N], BF16)
        lower = sb("lower", [P, DEPTH, N], BF16)
        acc_sb = sb("acc_sb", [P, NT, 2 * E], F32)
        rden = sb("hrden", [P, 2, NT], F32)
        h_out = sb("h_out", [P, NT, C], F32)
        x_res = sb("hx_res", [P, 2, 2, C], F32)
        stats = sb("hstats", [P, NT, 6], F32)
        meanvar = sb("hmeanvar", [P, NT, 2], F32)
        vareps = sb("hvareps", [P, NT], F32)
        rstd = sb("hrstd", [P, NT], F32)
        pause = sb("pause", [P, 2], F32)

        weighted = acc_sb[:, :, 0:E]
        negative = acc_sb[:, :, E:E + D]

        acc = ps("acc", [P, BANKS, CH])
        turn_ps = ps("turn_ps", [P, CH])
        q_ps = ps("q_ps", [P, CH])

        x_in_full = [sem(f"hx_in_full{k}") for k in range(4)]
        x_turned = sem("hx_turned")
        xT_full = sem("hxT_full")
        q_made = sem("q_made")
        q_full = sem("q_full")
        s_cols_full = sem("s_cols_full")
        s_turned = sem("s_turned")
        s_turned_full = sem("s_turned_full")
        s_stored = sem("s_stored")
        s_all_full = [sem(f"s_all_full{k}") for k in range(2)]
        s_all_free = sem("s_all_free")
        d_max_part = sem("d_max_part")
        d_max_full = sem("d_max_full")
        differences_full = sem("differences_full")
        d_huge_full = sem("d_huge_full")
        factors_full = sem("factors_full")
        s_sum_full = sem("s_sum_full")
        mean_made = sem("mean_made")
        mean_hi_full = sem("mean_hi_full")
        mean_full = sem("mean_full")
        values_full = sem("values_full")
        v_hi_full = sem("v_hi_full")
        v_lo_full = sem("v_lo_full")
        step_full = sem("step_full")
        upper_full = sem("upper_full")
        lower_full = sem("lower_full")
        edges_free = sem("edges_free")
        acc_made = sem("acc_made")
        acc_read = sem("acc_read")
        acc_scaled = sem("acc_scaled")
        weighted_full = sem("weighted_full")
        rden_full = sem("hrden_full")
        mixed_full = sem("mixed_full")
        negative_full = sem("negative_full")
        exp_full = sem("exp_full")
        elu_full = sem("elu_full")
        x_res_full = [sem(f"hx_res_full{k}") for k in range(2)]
        summed_full = sem("hsummed_full")
        stats_full = sem("hstats_full")
        meanvar_full = sem("hmeanvar_full")
        vareps_full = sem("hvareps_full")
        rstd_full = sem("hrstd_full")
        out_full = sem("out_full")
        out_stored = sem("out_stored")

        block = ctx.enter_context(nc.Block())

        def group(tile):
            return tile // GROUPS, tile % GROUPS * 2 * E

        @block.sync
        def _(sp):
            with sp.Fori(0, B) as b:
                with sp.Fori(0, NT // 4) as four:
                    for k in range(4):
                        t = NT * b + 4 * four + k
                        sp.wait_ge(x_turned, NT * b + 4 * four)
                        sp.dma_start(x_in[:, k, :], x1_rows[dynamic(t * P, P), :]).then_inc(x_in_full[k], 16)
                sp.wait_ge(s_turned_full, b + 1)
                sp.dma_start(s_rows[dynamic(b, 1), :, :].rearrange("o r n -> (o r) n"), s_turned_sb[:]).then_inc(s_stored, 16)
                sp.wait_ge(s_stored, 16 * b + 16)
                for h in range(H):
                    sp.wait_ge(s_all_free, H * b + h + 1)
                    row = s_rows[dynamic(b, 1), h * NT:(h + 1) * NT, :].rearrange("o r n -> (o r n)")
                    sp.dma_start(s_all[:, h % 2, :], row.partition_broadcast(P)).then_inc(s_all_full[h % 2], 16)

        @block.tensor
        def _(pe):
            pe.sem_inc(acc_read, BANKS)
            pe.sem_inc(edges_free, DEPTH)
            with pe.Fori(0, B) as b:
                with pe.Fori(0, NT // 4) as four:
                    for k in range(4):
                        t = NT * b + 4 * four + k
                        pe.wait_ge(x_in_full[k], 16 * (NT // 4 * b + four) + 16)
                        pe.wait_ge(xT_full, t)
                        for c in range(KC):
                            ins = nc.tensor.transpose(turn_ps[:, c * P:(c + 1) * P],
                                                      x_in[:, k, c * P:(c + 1) * P], ident[:])
                        ins.then_inc(x_turned, 1)
                        pe.wait_ge(xT_full, t + 1)
                        pe.wait_ge(q_full, t)
                        for c in range(KC):
                            ins = nc.tensor.matmul(q_ps[:, 0:Q], xT[:, k % 2, c, :], w_ext[:, c, :],
                                                   start=(c == 0), stop=(c == KC - 1))
                        ins.then_inc(q_made, 1)
                pe.wait_ge(s_cols_full, b + 1)
                pe.wait_ge(xT_full, NT * b + NT)
                pe.wait_ge(q_full, NT * b + NT)
                for t in range(NT):
                    ins = nc.tensor.matmul(q_ps[0:1, 0:C], st.mean_ones[:, 0:1], q[:, t, 0:C],
                                           start=(t == 0), stop=(t == NT - 1))
                    if t == 0:
                        nc.tensor.transpose(turn_ps[0:H * NT, 0:P], s_cols[:].rearrange("p h t -> p (h t)"),
                                            ident[:]).then_inc(s_turned, 1)
                ins.then_inc(mean_made, 1)
                pe.wait_ge(mean_full, b + 1)
                for h in range(H):
                    n = H * b + h
                    pe.wait_ge(v_lo_full, 2 * n + 2)
                    for tile in range(NT):
                        bank, at = group(tile)
                        if at == 0:
                            pe.wait_ge(acc_read, BANKS * n + bank + 1)
                        for m, mean in enumerate((mean_hi, mean_lo)):
                            nc.tensor.matmul(acc[:, bank, at:at + E], edgeless[0:1, tile * P:(tile + 1) * P],
                                             mean[0:1, h, :], start=(at == 0 and m == 0), stop=True,
                                             skip_group_check=True)
                    with pe.Fori(0, RUNS) as run:
                        for k in range(DEPTH):
                            j = DEPTH * run + k
                            jn = n * NT + j
                            pe.wait_ge(lower_full, jn + 1)
                            for tile in range(NT):
                                bank, at = group(tile)
                                for edges, hi, lo, col in ((upper, up_hi, up_lo, at), (lower, low_hi, low_lo, at + E)):
                                    for v in (hi, lo):
                                        ins = nc.tensor.matmul(
                                            acc[:, bank, col:col + E], edges[:, k, tile * P:(tile + 1) * P],
                                            v[:, h % 2, dynamic(j, 1), :], start=False, stop=True,
                                            skip_group_check=True)
                            ins.then_inc(edges_free, 1)
                    pe.wait_ge(edges_free, DEPTH + n * NT + NT)
                    pe.nop().then_inc(acc_made, 1)

        @block.scalar
        def _(act):
            def steps(b, h, run, tiles=range(DEPTH)):
                for k in tiles:
                    j = DEPTH * run + k
                    jn = (H * b + h) * NT + j
                    act.wait_ge(d_huge_full, 1)
                    act.wait_ge(edges_free, jn + 1)
                    nc.scalar.activation(upper[:, k, :], s_all[:, h % 2, :], ACT.Relu,
                                         bias=d_huge[:, dynamic(j, 1), h:h + 1].rearrange("p o h -> p (o h)")
                                         if not isinstance(j, int) else d_huge[:, j, h:h + 1],
                                         scale=HUGE).then_inc(step_full, 1)

            def split_values(b, h):
                for m, hi in enumerate((up_hi, low_hi)):
                    act.wait_ge(values_full, 2 * (H * b + h) + m + 1)
                    act.wait_ge(acc_made, H * b + max(h - 1, 0))
                    nc.scalar.activation(hi[:, h % 2, :, :], values[:, m, :, :], ACT.Copy).then_inc(v_hi_full, 1)

            def copy_acc(n):
                act.wait_ge(acc_made, n + 1)
                act.wait_ge(elu_full, n)
                for bank in range(BANKS):
                    tiles = min(GROUPS, NT - GROUPS * bank)
                    nc.scalar.activation(acc_sb[:, GROUPS * bank:GROUPS * bank + tiles, :].rearrange("p t e -> p (t e)"),
                                         acc[:, bank, 0:tiles * 2 * E], ACT.Copy).then_inc(acc_read, 1)

            def elu_exp(n):
                act.wait_ge(negative_full, n + 1)
                nc.scalar.activation(negative, negative, ACT.Exp).then_inc(exp_full, 1)

            act.sem_inc(s_all_free, 2)
            with act.Fori(0, B) as b:
                with act.Fori(0, NT // 4) as four:
                    for k in range(4):
                        t = NT * b + 4 * four + k
                        act.wait_ge(x_turned, t + 1)
                        act.wait_ge(q_made, NT * b + 4 * four) if k < 2 else act.wait_ge(q_made, t - 1)
                        nc.scalar.activation(xT[:, k % 2, :, :].rearrange("p c n -> p (c n)"), turn_ps[:, 0:C],
                                             ACT.Copy).then_inc(xT_full, 1)
                        act.wait_ge(x_turned, 1)
                        act.wait_ge(q_made, t + 1)
                        act.wait_ge(v_lo_full, 2 * H * b)
                        nc.scalar.activation(q[:, dynamic(4 * four + k, 1), :].rearrange("p o c -> p (o c)"),
                                             q_ps[:, 0:Q], ACT.Copy).then_inc(q_full, 1)
                act.wait_ge(s_turned, b + 1)
                act.wait_ge(s_stored, 16 * b)
                nc.scalar.activation(s_turned_sb[:], turn_ps[0:H * NT, 0:P], ACT.Copy).then_inc(s_turned_full, 1)
                act.wait_ge(differences_full, 2 * b + 2)
                act.wait_ge(weighted_full, H * b)
                nc.scalar.activation(up_factor[:], d_less[:], ACT.Exp).then_inc(factors_full, 1)
                nc.scalar.activation(low_factor[:], d_less[:], ACT.Exp, scale=ALPHA).then_inc(factors_full, 1)
                nc.scalar.activation(row_factor[:], s_more[:], ACT.Exp, scale=ALPHA - 1).then_inc(factors_full, 1)
                act.wait_ge(mean_made, b + 1)
                act.wait_ge(acc_made, H * b)
                nc.scalar.activation(mean_hi[0:1, :, 0:D], q_ps[0:1, 0:C].rearrange("p (h d) -> p h d", h=H),
                                     ACT.Copy).then_inc(mean_hi_full, 1)
                split_values(b, 0)
                act.wait_ge(d_huge_full, b + 1)
                for h in range(H):
                    n = H * b + h
                    act.wait_ge(s_all_full[h % 2], 16 * (H // 2 * b + h // 2) + 16)
                    steps(b, h, 0, range(DEPTH - 1))
                    if h > 0:
                        copy_acc(n - 1)
                    steps(b, h, 0, (DEPTH - 1,))
                    if RUNS // 2 > 1:
                        with act.Fori(1, RUNS // 2) as run:
                            steps(b, h, run)
                    if h > 0:
                        elu_exp(n - 1)
                    if h + 1 < H:
                        split_values(b, h + 1)
                    with act.Fori(RUNS // 2, RUNS) as run:
                        steps(b, h, run)
                    act.wait_ge(step_full, n * NT + NT)
                    act.sem_inc(s_all_free, 1)
                copy_acc(H * b + H - 1)
                elu_exp(H * b + H - 1)

        @block.gpsimd
        def _(pool):
            def make_values(b, h):
                n = H * b + h
                for m, factor in enumerate((up_factor, low_factor)):
                    pool.wait_ge(factors_full, 3 * b + 2)
                    pool.wait_ge(v_lo_full, 2 * n)
                    nc.gpsimd.tensor_tensor(values[:, m, :, 0:D], q[:, :, h * D:(h + 1) * D],
                                            factor[:, :, h:h + 1].to_broadcast([P, NT, D]),
                                            ALU.mult)
                    nc.gpsimd.tensor_tensor(values[:, m, :, D:E], factor[:, :, h:h + 1], st.den_scale[:, 0:1].unsqueeze(1).to_broadcast([P, NT, 1]),
                                            ALU.mult).then_inc(values_full, 1)
                for m, (hi, lo) in enumerate(((up_hi, up_lo), (low_hi, low_lo))):
                    pool.wait_ge(v_hi_full, 2 * n + m + 1)
                    nc.gpsimd.tensor_tensor(lo[:, h % 2, :, :], values[:, m, :, :], hi[:, h % 2, :, :],
                                            ALU.subtract).then_inc(v_lo_full, 1)

            with pool.Fori(0, B) as b:
                pool.wait_ge(d_max_part, b + 1)
                nc.gpsimd.tensor_tensor(pause[:, 0:1], st.minus_half[:], st.minus_half[:], ALU.add)
                nc.gpsimd.partition_all_reduce(d_max[:, 1, :], d_max[:, 0, :], P,
                                               bass.bass_isa.ReduceOp.max).then_inc(d_max_full, 1)
                make_values(b, 0)
                for h in range(H):
                    n = H * b + h
                    if h + 1 < H:
                        make_values(b, h + 1)
                    pool.wait_ge(acc_read, BANKS * (n + 2))
                    nc.gpsimd.tensor_tensor(acc_sb[:, :, E:2 * E], acc_sb[:, :, E:2 * E],
                                            row_factor[:, :, h:h + 1].to_broadcast([P, NT, E]),
                                            ALU.mult).then_inc(acc_scaled, 1)
                    pool.wait_ge(acc_scaled, n + 1)
                    nc.gpsimd.tensor_tensor(weighted, acc_sb[:, :, 0:E], acc_sb[:, :, E:2 * E],
                                            ALU.add).then_inc(weighted_full, 1)
                for two in range(NT // 2):
                    m = NT // 2 * b + two
                    if two < 2:
                        pool.wait_ge(summed_full, NT // 2 * b)
                    else:
                        pool.wait_ge(summed_full, m - 1)
                    rows = x1_rows[dynamic((NT * b + 2 * two) * P, 2 * P), :].rearrange("(t p) c -> p t c", p=P)
                    pool.dma_start(x_res[:, two % 2, :, :], rows).then_inc(x_res_full[two % 2], 16)
                pool.wait_ge(vareps_full, b + 1)
                nc.gpsimd.tensor_tensor(rstd[:], vareps[:], st.minus_half[:, 0:1].to_broadcast([P, NT]),
                                        ALU.pow).then_inc(rstd_full, 1)
                pool.wait_ge(out_full, b + 1)
                pool.dma_start(out_rows[dynamic(N * b, N), :].rearrange("(t p) c -> p t c", p=P),
                               h_out[:]).then_inc(out_stored, 16)
            pool.wait_ge(out_stored, 16 * B)

        @block.vector
        def _(dve):
            def edges(b, h, run):
                for two in range(0, DEPTH, 2):
                    tiles = []
                    for k in (two, two + 1):
                        j = DEPTH * run + k
                        jn = (H * b + h) * NT + j
                        adjacent = adjT[:, j, :] if isinstance(j, int) else \
                            adjT[:, dynamic(j, 1), :].rearrange("p o n -> p (o n)")
                        tiles.append((k, jn, adjacent))
                        dve.wait_ge(step_full, jn + 1)
                        nc.vector.tensor_tensor(upper[:, k, :], upper[:, k, :], adjacent,
                                                ALU.min).then_inc(upper_full, 1)
                    for k, jn, adjacent in tiles:
                        dve.wait_ge(upper_full, jn + 1)
                        nc.vector.tensor_tensor(lower[:, k, :], adjacent, upper[:, k, :],
                                                ALU.subtract).then_inc(lower_full, 1)

            def mix(b, h):
                n = H * b + h
                dve.wait_ge(weighted_full, n + 1)
                nc.vector.reciprocal(rden[:, 0, :], weighted[:, :, D:E].rearrange("p t o -> p (t o)")).then_inc(rden_full, 1)
                dve.wait_ge(rden_full, 2 * n + 1)
                nc.vector.tensor_scalar(rden[:, 1, :], rden[:, 0, :], st.unscale[:, 0:1], None, ALU.mult).then_inc(rden_full, 1)
                dve.wait_ge(rden_full, 2 * n + 2)
                dve.wait_ge(out_stored, 16 * b)
                nc.vector.tensor_tensor(h_out[:, :, h * D:(h + 1) * D], weighted[:, :, 0:D],
                                        rden[:, 1, :].unsqueeze(2).to_broadcast([P, NT, D]),
                                        ALU.mult).then_inc(mixed_full, 1)
                dve.wait_ge(mixed_full, n + 1)
                nc.vector.tensor_scalar(negative, h_out[:, :, h * D:(h + 1) * D], 0.0, None,
                                        ALU.min).then_inc(negative_full, 1)

            def elu(b, h):
                n = H * b + h
                dve.wait_ge(exp_full, n + 1)
                nc.vector.scalar_tensor_tensor(out=h_out[:, :, h * D:(h + 1) * D], in0=h_out[:, :, h * D:(h + 1) * D],
                                               scalar=0.0, in1=negative, op0=ALU.max,
                                               op1=ALU.add).then_inc(elu_full, 1)

            with dve.Fori(0, B) as b:
                dve.wait_ge(q_full, NT * b + NT)
                dve.wait_ge(s_turned, b)
                nc.vector.tensor_copy(s_cols[:], q[:, :, C:C + H].rearrange("p t h -> p h t")).then_inc(s_cols_full, 1)
                nc.vector.tensor_reduce(d_max[:, 0, :], q[:, :, C + H:Q].rearrange("p t h -> p h t"), AX.X,
                                        ALU.max).then_inc(d_max_part, 1)
                dve.wait_ge(step_full, H * NT * b)
                nc.vector.tensor_scalar(d_huge[:], q[:, :, C + H:Q], HUGE, None, ALU.mult).then_inc(d_huge_full, 1)
                dve.wait_ge(d_max_full, b + 1)
                dve.wait_ge(factors_full, 3 * b)
                top = d_max[:, 1, :].unsqueeze(1).to_broadcast([P, NT, H])
                nc.vector.tensor_tensor(d_less[:], q[:, :, C + H:Q], top, ALU.subtract).then_inc(differences_full, 1)
                nc.vector.tensor_tensor(s_more[:], q[:, :, C:C + H], top, ALU.add).then_inc(s_sum_full, 1)
                dve.wait_ge(s_sum_full, b + 1)
                nc.vector.tensor_scalar(s_more[:], s_more[:], 0.0, None, ALU.max).then_inc(differences_full, 1)
                dve.wait_ge(mean_hi_full, b + 1)
                nc.vector.tensor_tensor(mean_lo[0:1, :, 0:D], q_ps[0:1, 0:C].rearrange("p (h d) -> p h d", h=H),
                                        mean_hi[0:1, :, 0:D], ALU.subtract).then_inc(mean_full, 1)
                for h in range(H):
                    edges(b, h, 0)
                    if RUNS // 2 > 1:
                        with dve.Fori(1, RUNS // 2) as run:
                            edges(b, h, run)
                    if h > 0:
                        mix(b, h - 1)
                    if h > 0:
                        elu(b, h - 1)
                    with dve.Fori(RUNS // 2, RUNS) as run:
                        edges(b, h, run)
                mix(b, H - 1)
                elu(b, H - 1)
                dve.wait_ge(elu_full, H * b + H)
                for two in range(NT // 2):
                    dve.wait_ge(x_res_full[two % 2], 16 * (NT // 4 * b + two // 2) + 16)
                    pair_out = h_out[:, 2 * two:2 * two + 2, :].rearrange("p t c -> p (t c)")
                    nc.vector.scalar_tensor_tensor(out=pair_out, in0=pair_out, scalar=-1.0,
                                                   in1=x_res[:, two % 2, :, :].rearrange("p t c -> p (t c)"),
                                                   op0=ALU.add, op1=ALU.add).then_inc(summed_full, 1)
                dve.wait_ge(summed_full, NT // 2 * (b + 1))
                for t in range(NT):
                    nc.vector.bn_stats(stats[:, t, :], h_out[:, t, :]).then_inc(stats_full, 1)
                dve.wait_ge(stats_full, NT * (b + 1))
                nc.vector.memset(pause[:, 1:2], 0.0)
                for t in range(NT):
                    nc.vector.bn_aggr(meanvar[:, t, :], stats[:, t, :]).then_inc(meanvar_full, 1)
                dve.wait_ge(meanvar_full, NT * (b + 1))
                nc.vector.tensor_scalar(vareps[:], meanvar[:, :, 1:2].rearrange("p t o -> p (t o)"), EPS, None,
                                        ALU.add).then_inc(vareps_full, 1)
                dve.wait_ge(rstd_full, b + 1)
                for t in range(NT):
                    ins = nc.vector.tensor_scalar(h_out[:, t, :], h_out[:, t, :], meanvar[:, t, 0:1], rstd[:, t:t + 1],
                                                  ALU.subtract, ALU.mult)
                ins.then_inc(out_full, 1)


class Store:
    pass


def bass_two_graph_layers(nc, x, adj, W1, W2, W3, W, a, out):
    B, N, C = x.shape
    x1 = nc.dram_tensor("x1", x.shape, F32, kind="Internal").ap()
    s_rows = nc.dram_tensor("s_rows", (B, N // P * (C // (a.shape[0] // 2)), P), F32, kind="Internal").ap()
    st = Store()
    with ExitStack() as ctx:
        def sb(name, shape, dt):
            return ctx.enter_context(nc.sbuf_tensor(name, shape, dt))

        st.ident = sb("ident", [P, P], F32)
        st.minus_half = sb("minus_half", [P, 1], F32)
        mask = ctx.enter_context(ExitStack())
        st.notadj = mask.enter_context(nc.sbuf_tensor("notadj", [P, N // P, N], U8, side="right"))
        with ExitStack() as dense:
            def sd(name, shape, dt):
                return dense.enter_context(nc.sbuf_tensor(name, shape, dt))
            st.w3 = sd("w3", [P, 2, C], F32)
            st.a_hi = sd("a_hi", [P, 2, C], F32R)
            st.a_lo = sd("a_lo", [P, 2, C], F32R)
            st.h3_hi = sd("h3_hi", [P, 2 * (N // P), C + 1], F16)
            build_setup(nc, st, W1, W2, W3)
            build_dense(nc, st, x, adj, x1)
        NT = N // P
        H = C // (a.shape[0] // 2)
        E = C // H + 1
        st.adjT = sb("adjT", [P, NT, N], BF16)
        st.edgeless = sb("edgeless", [1, N], BF16)
        st.w_ext = sb("w_ext", [P, C // P, C + 2 * H], F32)
        st.unscale = sb("unscale", [P, 1], F32)
        st.den_scale = sb("den_scale", [P, 1], F32)
        st.mean_ones = sb("mean_ones", [P, 1], F32)
        st.mean_hi = sb("mean_hi", [1, H, E], F16)
        st.mean_lo = sb("mean_lo", [1, H, E], F16)
        build_edges(nc, st, W, a)
        mask.close()
        build_heads(nc, st, x1, s_rows, out)


_INS = ["x", "adj", "L0_gnn_W1", "L0_gnn_W2", "L0_gnn_W3", "L1_gnn_W", "L1_gnn_a"]


def kernel(**inputs):
    import numpy as _np
    import concourse.bacc as _bacc
    from concourse import mybir as _mybir
    from concourse.bass_utils import run_bass_kernel_spmd as _run

    nc = _bacc.Bacc("TRN2", target_bir_lowering=False, num_devices=1)
    arrays, args = {}, []
    for name in _INS:
        a = _np.ascontiguousarray(inputs[name])
        arrays[f"in_{name}_dram"] = a
        args.append(nc.dram_tensor(f"in_{name}_dram", a.shape, _mybir.dt.from_np(a.dtype), kind="ExternalInput").ap())
    shape = inputs["x"].shape
    args.append(nc.dram_tensor("out_0_dram", shape, _mybir.dt.float32, kind="ExternalOutput").ap())
    bass_two_graph_layers(nc, *args)
    r = _run(nc, [arrays], core_ids=[0])
    return r.results[0]["out_0_dram"]
```

```python
from contextlib import ExitStack

import concourse.bass as bass
from concourse import mybir

P = 128
F32 = mybir.dt.float32
F32R = mybir.dt.float32r
F16 = mybir.dt.float16
BF16 = mybir.dt.bfloat16
U8 = mybir.dt.uint8
I32 = mybir.dt.int32
ALU = mybir.AluOpType
ACT = mybir.ActivationFunctionType
AX = mybir.AxisListType

ALPHA = 0.2
EPS = 1e-5
MASKED = -1e30
LN_1024 = 6.931471805599453
CH = 512
TB = CH // P
HUGE = 2.0 ** 100
Q_SCALE = 2048.0
DEN_SCALE = 1024.0


def dynamic(start, size):
    return bass.ds(start, size)


class Fresh:

    def __init__(self, engine, name, largest):
        self.engine, self.register, self.largest = engine, engine.alloc_register(name), largest

    def __call__(self, value):
        if isinstance(value, int):
            return value
        self.engine.reg_mov(self.register, value)
        return self.engine.snap(self.register, min_val=0, max_val=self.largest)


def build_setup(nc, st, W1, W2, W3):
    ident, w3, a_hi, a_lo = st.ident, st.w3, st.a_hi, st.a_lo
    with ExitStack() as ctx:
        w1 = ctx.enter_context(nc.sbuf_tensor("w1_rows", [P, 2, 256], F32))
        w2 = ctx.enter_context(nc.sbuf_tensor("w2_rows", [P, 2, 256], F32))
        w1T = ctx.enter_context(nc.sbuf_tensor("w1T", [P, 2, 256], F32))
        w2T = ctx.enter_context(nc.sbuf_tensor("w2T", [P, 2, 256], F32))
        turned = ctx.enter_context(nc.psum_tensor("w_turned", [P, 4, CH], F32))
        a_ps = ctx.enter_context(nc.psum_tensor("a_ps", [P, 2, CH], F32))
        w_loaded = ctx.enter_context(nc.semaphore("w_loaded"))
        ident_zero = ctx.enter_context(nc.semaphore("ident_zero"))
        ident_ready = ctx.enter_context(nc.semaphore("ident_ready"))
        w_turned = ctx.enter_context(nc.semaphore("w_turned_ready"))
        wT_ready = ctx.enter_context(nc.semaphore("wT_ready"))
        a_ready = ctx.enter_context(nc.semaphore("a_ready"))
        a_hi_ready = ctx.enter_context(nc.semaphore("a_hi_ready"))
        block = ctx.enter_context(nc.Block())

        @block.sync
        def _(sp):
            for dst, src in ((w1, W1), (w2, W2), (w3, W3)):
                sp.dma_start(dst[:], src.rearrange("(k p) d -> p k d", p=P)).then_inc(w_loaded, 16)
            sp.wait_ge(w_loaded, 48)

        @block.gpsimd
        def _(pool):
            nc.gpsimd.memset(ident[:], 0.0).then_inc(ident_zero, 1)
            nc.gpsimd.memset(st.minus_half[:], -0.5)
            pool.wait_ge(ident_zero, 1)
            nc.gpsimd.affine_select(out=ident[:], in_=ident[:], compare_op=ALU.not_equal, fill=1.0,
                                    base=0, pattern=[[-1, P]], channel_multiplier=1).then_inc(ident_ready, 1)

        @block.tensor
        def _(pe):
            pe.wait_ge(w_loaded, 48)
            pe.wait_ge(ident_ready, 1)
            for n, w in enumerate((w1, w2)):
                for dk in range(2):
                    for ck in range(2):
                        ins = nc.tensor.transpose(turned[:, 2 * n + dk, ck * P:(ck + 1) * P],
                                                  w[:, ck, dk * P:(dk + 1) * P], ident[:])
            ins.then_inc(w_turned, 1)
            pe.wait_ge(wT_ready, 4)
            for ck in range(2):
                for dk in range(2):
                    ins = nc.tensor.matmul(a_ps[:, ck, 0:256], w1T[:, dk, ck * P:(ck + 1) * P],
                                           w2T[:, dk, :], start=(dk == 0), stop=(dk == 1))
            ins.then_inc(a_ready, 1)

        @block.vector
        def _(dve):
            dve.wait_ge(w_turned, 1)
            for n, wT in enumerate((w1T, w2T)):
                for dk in range(2):
                    nc.vector.tensor_copy(wT[:, dk, :], turned[:, 2 * n + dk, 0:256]).then_inc(wT_ready, 1)
            dve.wait_ge(a_ready, 1)
            for ck in range(2):
                nc.vector.tensor_copy(a_hi[:, ck, :], a_ps[:, ck, 0:256]).then_inc(a_hi_ready, 1)
            dve.wait_ge(a_hi_ready, 2)
            for ck in range(2):
                nc.vector.tensor_tensor(a_lo[:, ck, :], a_ps[:, ck, 0:256],
                                        a_hi[:, ck, :].bitcast(F32), ALU.subtract)
            nc.vector.memset(st.h3_hi[:, :, 256:257], 1.0)


def build_dense(nc, st, x, adj, x1):
    B, N, C = x.shape
    NB = N // CH
    NT = N // P
    BLOCKS = B * NB
    SLOTS = 2 * NB
    KC = C // P
    ALL = B * NT
    x_rows = x.rearrange("b n c -> (b n) c")
    x1_rows = x1.rearrange("b n c -> (b n) c")
    ident, w3, a_hi, a_lo, notadj, h3_hi = st.ident, st.w3, st.a_hi, st.a_lo, st.notadj, st.h3_hi
    PREP_AT = {0: (0, 1), 1: (2,), 2: (3,), 3: ()}
    Y_AT = {0: 0, 1: 1}
    Y_SPLIT_AT = 2
    TURN_AT = {NB // 2 - 1: 0, NB // 2: 1}

    with ExitStack() as ctx:
        def sb(name, shape, dt):
            return ctx.enter_context(nc.sbuf_tensor(name, shape, dt))

        def ps(name, shape, dt=F32):
            return ctx.enter_context(nc.psum_tensor(name, shape, dt))

        def sem(name):
            return ctx.enter_context(nc.semaphore(name))

        xT_hi = sb("xT_hi", [P, SLOTS, KC, CH], F32R)
        xT_lo = sb("xT_lo", [P, SLOTS, KC, CH], F32R)
        h3_lo = sb("h3_lo", [P, 2 * NT, C], F16)
        y_raw = sb("y_raw", [P, KC, CH], F32)
        y_hi = sb("y_hi", [P, KC, CH], F32R)
        y_lo = sb("y_lo", [P, KC, CH], F32R)
        relu_e = sb("relu_e", [P, N], F32)
        probs = sb("probs", [P, 2, N], F32)
        pT_hi = sb("pT_hi", [P, TB, CH], F16)
        pT_lo = sb("pT_lo", [P, TB, CH], F16)
        x_in = sb("x_in", [P, TB, C], F32)
        x_res = sb("x_res", [P, TB, C], F32)
        xT_raw = sb("xT_raw", [P, 2, KC, P], F32)
        gat = sb("gat", [P, 2, C], F32)
        summed = sb("summed", [P, 2, C], F32)
        x1_out = sb("x1_out", [P, TB, C], F32)
        bankmax = sb("bankmax", [P, 2, NB], F32)
        rowmax = sb("rowmax", [P, 2], F32)
        shift = sb("shift", [P, 2], F32)
        rden = sb("rden", [P, 2], F32)
        stats = sb("stats", [P, 2, 6], F32)
        meanvar = sb("meanvar", [P, 2, 2], F32)
        vareps = sb("vareps", [P, 2], F32)
        rstd = sb("rstd", [P, 2], F32)
        adj_in = sb("adj_in", [P, N], I32)

        e_ps = ps("e_ps", [P, NB, CH])
        pT_ps = ps("pT_ps", [P, 2, CH])
        out_ps = ps("out_ps", [P, CH])
        misc_ps = ps("misc_ps", [P, CH])

        x_in_full = [sem(f"x_in_full{k}") for k in range(TB)]
        x_res_full = [sem(f"x_res_full{k}") for k in range(TB)]
        x1_stored = [sem(f"x1_stored{k}") for k in range(TB)]
        adj_full = sem("adj_full")
        mask_made = sem("mask_made")
        xT_turned = sem("xT_turned")
        xT_raw_full = sem("xT_raw_full")
        xT_hi_full = sem("xT_hi_full")
        xT_lo_full = sem("xT_lo_full")
        h3_made = sem("h3_made")
        h3_hi_full = sem("h3_hi_full")
        h3_lo_full = sem("h3_lo_full")
        y_made = sem("y_made")
        y_raw_full = sem("y_raw_full")
        y_hi_full = sem("y_hi_full")
        y_lo_full = sem("y_lo_full")
        e_made = sem("e_made")
        relu_e_full = sem("relu_e_full")
        edges_full = sem("edges_full")
        masked_full = sem("masked_full")
        rowmax_full = sem("rowmax_full")
        shift_full = sem("shift_full")
        probs_full = sem("probs_full")
        pT_turned = sem("pT_turned")
        pT_hi_full = sem("pT_hi_full")
        pT_lo_full = sem("pT_lo_full")
        pv_made = sem("pv_made")
        rden_full = sem("rden_full")
        gat_full = sem("gat_full")
        summed_full = sem("summed_full")
        stats_full = sem("stats_full")
        meanvar_full = sem("meanvar_full")
        vareps_full = sem("vareps_full")
        rstd_full = sem("rstd_full")
        x1_full = sem("x1_full")

        block = ctx.enter_context(nc.Block())

        runs = [(1, NB - 1, True, True), (NB - 1, BLOCKS - NB, False, True),
                (BLOCKS - NB, BLOCKS - 1, False, False)]

        def over_blocks(engine, step):
            step(0, True, True, True)
            for first, end, masks, preps in runs:
                if first < end:
                    with engine.Fori(first, end) as it:
                        step(it, masks, preps, True)
            step(BLOCKS - 1, False, False, False)

        def preps_before(it, preps):
            return NT + TB * it if preps else ALL

        def prep_slot(it):
            return (it + NB) % SLOTS

        def batch_slot(it):
            return (it // NB) % 2 * NB

        @block.sync
        def _(sp):
            def load_adj(tile, n):
                if not (isinstance(n, int) and n == 0):
                    sp.wait_ge(mask_made, n)
                sp.dma_start(adj_in[:], adj[dynamic(tile * P, P), :]).then_inc(adj_full, 16)

            def load_x(row_tile, k, n):
                if not (isinstance(n, int) and n <= 0):
                    sp.wait_ge(xT_turned, n)
                sp.dma_start(x_in[:, k, :], x_rows[dynamic(row_tile * P, P), :]).then_inc(x_in_full[k], 16)

            for k in range(TB):
                load_x(k, k, 0)
            load_adj(0, 0)
            with sp.Fori(1, NB) as j:
                for k in range(TB):
                    load_x(TB * j + k, k, TB * j - TB + k + 1)
            for k in range(1, TB):
                load_adj(k, k)

            def load_residual(it, k):
                sp.dma_start(x_res[:, k, :], x_rows[dynamic((TB * it + k) * P, P), :]).then_inc(x_res_full[k], 16)

            def step(it, masks, next_preps, more):
                for k in range(TB):
                    if masks:
                        load_adj(TB * it + TB + k, TB * it + TB + k)
                    sp.wait_ge(x1_full, TB * it + k + 1)
                    sp.dma_start(x1_rows[dynamic((TB * it + k) * P, P), :], x1_out[:, k, :]).then_inc(x1_stored[k], 16)
                    if more:
                        load_residual(it + 1, k)
                    if next_preps and k == TB - 2:
                        for m in range(TB):
                            load_x(NT + TB * (it + 1) + m, m, NT + TB * it + m + 1)

            for k in range(TB):
                load_residual(0, k)
            for k in range(TB):
                load_x(NT + k, k, NT - TB + k + 1)
            step(0, True, True, True)
            for first, end, masks, next_preps in ((1, NB - 1, True, True), (NB - 1, BLOCKS - NB - 1, False, True),
                                                  (BLOCKS - NB - 1, BLOCKS - 1, False, False)):
                if first < end:
                    with sp.Fori(first, end) as it:
                        step(it, masks, next_preps, True)
            step(BLOCKS - 1, False, False, False)
            for k in range(TB):
                sp.wait_ge(x1_stored[k], 16 * BLOCKS)

        @block.tensor
        def _(pe):
            fresh_slot = Fresh(pe, "fresh_slot", NB)

            def turn_x(n, k, round_):
                pe.wait_ge(x_in_full[k], 16 * round_)
                if not (isinstance(n, int) and n == 0):
                    pe.wait_ge(h3_lo_full, n)
                for c in range(KC):
                    ins = nc.tensor.transpose(misc_ps[:, c * P:(c + 1) * P],
                                              x_in[:, k, c * P:(c + 1) * P], ident[:])
                ins.then_inc(xT_turned, 1)

            def make_h3(n, k):
                pe.wait_ge(xT_raw_full, n + 1)
                for c in range(KC):
                    ins = nc.tensor.matmul(misc_ps[:, 0:C], xT_raw[:, k % 2, c, :], w3[:, c, :],
                                           start=(c == 0), stop=(c == KC - 1))
                ins.then_inc(h3_made, 1)

            def make_y(half, slot):
                passes = [(a, xt) for a, xt in ((a_hi, xT_hi), (a_hi, xT_lo), (a_lo, xT_hi))]
                for c in range(KC):
                    for m, (a, xt) in enumerate(passes):
                        ins = nc.tensor.matmul(misc_ps[:], a[:, c, half * P:(half + 1) * P],
                                               xt[:, slot, c, :] if isinstance(slot, int)
                                               else xt[:, dynamic(slot, 1), c, :],
                                               start=(c == 0 and m == 0),
                                               stop=(c == KC - 1 and m == len(passes) - 1))
                ins.then_inc(y_made, 1)

            def make_e(tile, k, base, between=None):
                base = fresh_slot(base)
                passes = ((y_hi, xT_hi), (y_hi, xT_lo), (y_lo, xT_hi))
                for bank in range(NB):
                    if not (isinstance(tile, int) and tile == 0):
                        pe.wait_ge(masked_full, NB * tile - NB + bank + 1)
                    for c in range(KC):
                        for m, (y, xt) in enumerate(passes):
                            ins = nc.tensor.matmul(e_ps[:, bank, :], y[:, c, k * P:(k + 1) * P],
                                                   xt[:, dynamic(base + bank, 1), c, :],
                                                   start=(c == 0 and m == 0),
                                                   stop=(c == KC - 1 and m == len(passes) - 1))
                    ins.then_inc(e_made, 1)
                    if between and bank in TURN_AT:
                        between(TURN_AT[bank])

            def turn_p(tile, k, c):
                if c == 0:
                    pe.wait_ge(probs_full, tile + 1)
                n = NB * tile + c - 1
                if not (isinstance(n, int) and n <= 0):
                    pe.wait_ge(pT_lo_full, n)
                for m in range(TB):
                    ins = nc.tensor.transpose(pT_ps[:, c % 2, m * P:(m + 1) * P],
                                              probs[:, k % 2, (TB * c + m) * P:(TB * c + m + 1) * P],
                                              ident[:])
                ins.then_inc(pT_turned, 1)

            def make_pv(tile, k, c, base):
                pe.wait_ge(pT_lo_full, NB * tile + c + 1)
                base = fresh_slot(base)
                if c == 0 and not (isinstance(tile, int) and tile == 0):
                    pe.wait_ge(gat_full, tile)
                for m in range(TB):
                    j = base * TB + TB * c + m
                    hi, lo = h3_hi[:, dynamic(j, 1), :], h3_lo[:, dynamic(j, 1), :]
                    first = c == 0 and m == 0
                    last = c == NB - 1 and m == TB - 1
                    w_hi = pT_hi[:, c, m * P:(m + 1) * P]
                    w_lo = pT_lo[:, c, m * P:(m + 1) * P]
                    nc.tensor.matmul(out_ps[:, 0:C + 1], w_hi, hi, start=first, stop=False)
                    nc.tensor.matmul(out_ps[:, 0:C], w_hi, lo, start=False, stop=False)
                    ins = nc.tensor.matmul(out_ps[:, 0:C + 1], w_lo, hi, start=False, stop=last)
                ins.then_inc(pv_made, 1)

            for k in range(TB):
                turn_x(k, k, 1)
                make_h3(k, k)
            with pe.Fori(1, NB) as j:
                for k in range(TB):
                    turn_x(TB * j + k, k, j + 1)
                    make_h3(TB * j + k, k)
            pe.wait_ge(h3_lo_full, NT)
            pe.wait_ge(xT_lo_full, NT)
            make_y(0, 0)
            pe.wait_ge(y_raw_full, 1)
            make_y(1, 0)
            pe.wait_ge(y_lo_full, 1)
            make_e(0, 0, 0)

            def step(it, masks, preps, more):
                n = preps_before(it, preps)
                tile = TB * it
                base = batch_slot(it)
                for k in range(TB):
                    todo = list(PREP_AT[k]) if preps else []
                    made = sum(len(PREP_AT[i]) for i in range(k)) if preps else 0
                    if todo:
                        pe.wait_ge(y_raw_full, 2 * it + 2 + sum(i < k for i in Y_AT))
                        turn_x(n + made, todo[0], NB + it + 1)

                    def first_turns(c, tile=tile, k=k):
                        turn_p(tile + k, k, c)

                    if k < TB - 1:
                        make_e(tile + k + 1, k + 1, base, first_turns)
                    elif more:
                        pe.wait_ge(y_lo_full, it + 2)
                        pe.wait_ge(xT_lo_full, n + (TB if preps else 0))
                        make_e(tile + TB, 0, batch_slot(it + 1), first_turns)
                    else:
                        first_turns(0)
                        first_turns(1)
                    if todo:
                        make_h3(n + made, todo[0])
                    for c in range(NB):
                        make_pv(tile + k, k, c, base)
                        if c + 2 < NB:
                            turn_p(tile + k, k, c + 2)
                        if c == 0 and len(todo) > 1:
                            turn_x(n + made + 1, todo[1], NB + it + 1)
                        if c == 1 % NB and len(todo) > 1:
                            make_h3(n + made + 1, todo[1])
                        if c == NB - 1 and more and k in Y_AT:
                            done = made + len(todo)
                            pe.wait_ge(h3_lo_full, n + done)
                            pe.wait_ge(xT_lo_full, n)
                            pe.wait_ge(y_raw_full, 2 * it + 2 + sum(i < k for i in Y_AT))
                            make_y(Y_AT[k], (it + 1) % SLOTS)

            over_blocks(pe, step)

        @block.scalar
        def _(act):
            def copy_xT(n, k):
                act.wait_ge(xT_turned, n + 1)
                if not (isinstance(n, int) and n < 2):
                    act.wait_ge(h3_made, n - 1)
                    act.wait_ge(xT_lo_full, n - 1)
                nc.scalar.activation(xT_raw[:, k % 2, :, :].rearrange("p c n -> p (c n)"), misc_ps[:, 0:C],
                                     ACT.Copy).then_inc(xT_raw_full, 1)

            def copy_h3(n, k, slot, pv):
                act.wait_ge(h3_made, n + 1)
                if pv is not None:
                    act.wait_ge(pv_made, pv)
                nc.scalar.activation(h3_hi[:, dynamic(slot * TB + k, 1), 0:C], misc_ps[:, 0:C],
                                     ACT.Copy).then_inc(h3_hi_full, 1)

            def copy_y(half, n):
                act.wait_ge(y_made, n + 1)
                if not (isinstance(n, int) and n < 2):
                    act.wait_ge(y_lo_full, (n - half) // 2 if isinstance(n, int) else n)
                nc.scalar.activation(y_raw[:, half, :], misc_ps[:], ACT.Copy).then_inc(y_raw_full, 1)

            def split_y(blocks):
                act.wait_ge(y_raw_full, 2 * blocks + 2)
                if not (isinstance(blocks, int) and blocks == 0):
                    act.wait_ge(e_made, NB * TB * blocks)
                nc.scalar.activation(y_hi[:], y_raw[:], ACT.Copy).then_inc(y_hi_full, 1)

            def positive_part(tile, between=None):
                for bank in range(NB):
                    act.wait_ge(e_made, NB * tile + bank + 1)
                    if not (isinstance(tile, int) and tile == 0):
                        act.wait_ge(masked_full, NB * tile - NB + bank + 1)
                    nc.scalar.activation(relu_e[:, bank * CH:(bank + 1) * CH], e_ps[:, bank, :], ACT.Relu,
                                         scale=1 / ALPHA - 1).then_inc(relu_e_full, 1)
                    if between and bank in TURN_AT:
                        between(TURN_AT[bank])

            def exponentials(tile, k):
                act.wait_ge(shift_full, tile + 1)
                nc.scalar.activation(probs[:, k % 2, :], probs[:, k % 2, :], ACT.Exp,
                                     bias=shift[:, k % 2:k % 2 + 1]).then_inc(probs_full, 1)

            def copy_pT(tile, c):
                act.wait_ge(pT_turned, NB * tile + c + 1)
                n = NB * tile + c - NB + 1
                if not (isinstance(n, int) and n <= 0):
                    act.wait_ge(pv_made, n)
                nc.scalar.activation(pT_hi[:, c, :], pT_ps[:, c % 2, :], ACT.Copy).then_inc(pT_hi_full, 1)

            def relu(tile, k):
                act.wait_ge(rden_full, tile + 1)
                if not (isinstance(tile, int) and tile < 2):
                    act.wait_ge(summed_full, tile - 1)
                nc.scalar.activation(gat[:, k % 2, :], out_ps[:, 0:C], ACT.Relu,
                                     scale=rden[:, k % 2:k % 2 + 1]).then_inc(gat_full, 1)

            for k in range(TB):
                copy_xT(k, k)
                copy_h3(k, k, 0, None)
            with act.Fori(1, NB) as j:
                for k in range(TB):
                    copy_xT(TB * j + k, k)
                    copy_h3(TB * j + k, k, j, None)
            copy_y(0, 0)
            copy_y(1, 1)
            split_y(0)
            positive_part(0)
            exponentials(0, 0)

            def step(it, masks, preps, more):
                n = preps_before(it, preps)
                tile = TB * it
                for k in range(TB):
                    todo = list(PREP_AT[k]) if preps else []
                    made = sum(len(PREP_AT[i]) for i in range(k)) if preps else 0
                    if todo:
                        copy_xT(n + made, todo[0])

                    def first_copies(c, tile=tile, k=k):
                        copy_pT(tile + k, c)

                    if k < TB - 1 or more:
                        positive_part(tile + k + 1, first_copies)
                    else:
                        first_copies(0)
                        first_copies(1)
                    if k == Y_SPLIT_AT and more:
                        split_y(it + 1)
                    if todo:
                        copy_h3(n + made, todo[0], prep_slot(it), NB * tile)
                    for c in range(2, NB):
                        copy_pT(tile + k, c)
                        if c == 2 and len(todo) > 1:
                            copy_xT(n + made + 1, todo[1])
                    if NB == 2 and len(todo) > 1:
                        copy_xT(n + made + 1, todo[1])
                    if len(todo) > 1:
                        copy_h3(n + made + 1, todo[1], prep_slot(it), NB * tile)
                    if k < TB - 1 or more:
                        exponentials(tile + k + 1, k + 1)
                    if more and k in Y_AT:
                        act.wait_ge(y_made, 2 * it + 3 + Y_AT[k])
                        if Y_AT[k] == 0:
                            act.wait_ge(y_lo_full, it + 1)
                        nc.scalar.activation(y_raw[:, Y_AT[k], :], misc_ps[:], ACT.Copy).then_inc(y_raw_full, 1)
                    relu(tile + k, k)

            over_blocks(act, step)

        @block.vector
        def _(dve):
            def make_mask(n):
                dve.wait_ge(adj_full, 16 * (n + 1))
                dst = notadj[:, n, :] if isinstance(n, int) else notadj[:, dynamic(n, 1), :]
                nc.vector.tensor_scalar(dst, adj_in[:], 0.0, None, ALU.is_le).then_inc(mask_made, 1)

            def split_xT(n, k, slot, scores):
                dve.wait_ge(xT_raw_full, n + 1)
                if scores is not None:
                    dve.wait_ge(e_made, scores)
                raw = xT_raw[:, k % 2, :, :]
                hi = xT_hi[:, dynamic(slot, 1), :, k * P:(k + 1) * P].rearrange("p o c n -> p (o c) n")
                lo = xT_lo[:, dynamic(slot, 1), :, k * P:(k + 1) * P].rearrange("p o c n -> p (o c) n")
                nc.vector.tensor_copy(hi, raw).then_inc(xT_hi_full, 1)
                dve.wait_ge(xT_hi_full, n + 1)
                nc.vector.tensor_tensor(lo, raw, hi.bitcast(F32), ALU.subtract).then_inc(xT_lo_full, 1)

            def split_h3(n, k, slot):
                dve.wait_ge(h3_hi_full, n + 1)
                j = slot * TB + k
                nc.vector.tensor_tensor(h3_lo[:, dynamic(j, 1), :].rearrange("p o c -> p (o c)"), misc_ps[:, 0:C],
                                        h3_hi[:, dynamic(j, 1), 0:C].rearrange("p o c -> p (o c)"),
                                        ALU.subtract).then_inc(h3_lo_full, 1)

            def split_y(blocks):
                dve.wait_ge(y_hi_full, blocks + 1)
                nc.vector.tensor_tensor(y_lo[:], y_raw[:], y_hi[:].bitcast(F32), ALU.subtract).then_inc(y_lo_full, 1)

            def mask(tile, k, row_tile, between=None):
                if not (isinstance(tile, int) and tile < 2):
                    dve.wait_ge(pT_turned, NB * tile - NB)
                for bank in range(NB):
                    cols = slice(bank * CH, (bank + 1) * CH)
                    dve.wait_ge(relu_e_full, NB * tile + bank + 1)
                    nc.vector.scalar_tensor_tensor(
                        out=relu_e[:, cols], in0=notadj[:, dynamic(row_tile, 1), cols].rearrange("p o n -> p (o n)"),
                        scalar=MASKED, in1=relu_e[:, cols], op0=ALU.mult, op1=ALU.add).then_inc(edges_full, 1)
                    dve.wait_ge(edges_full, 1)
                    dve.wait_ge(edges_full, NB * tile + bank + 1)
                    nc.vector.tensor_tensor_reduce(
                        out=probs[:, k % 2, cols], in0=e_ps[:, bank, :], in1=relu_e[:, cols], scale=ALPHA,
                        scalar=-3e38, op0=ALU.add, op1=ALU.max,
                        accum_out=bankmax[:, k % 2, bank:bank + 1]).then_inc(masked_full, 1)
                    if between and bank in TURN_AT:
                        between(TURN_AT[bank])

            def maximum(tile, k):
                dve.wait_ge(masked_full, NB * tile + NB)
                nc.vector.tensor_reduce(rowmax[:, k % 2:k % 2 + 1], bankmax[:, k % 2, :], AX.X,
                                        ALU.max).then_inc(rowmax_full, 1)
                dve.wait_ge(rowmax_full, tile + 1)
                if not (isinstance(tile, int) and tile < 2):
                    dve.wait_ge(probs_full, tile - 1)
                nc.vector.tensor_scalar(shift[:, k % 2:k % 2 + 1], rowmax[:, k % 2:k % 2 + 1], -1.0, LN_1024,
                                        ALU.mult, ALU.add).then_inc(shift_full, 1)

            def split_pT(tile, c):
                dve.wait_ge(pT_hi_full, NB * tile + c + 1)
                nc.vector.tensor_tensor(pT_lo[:, c, :], pT_ps[:, c % 2, :], pT_hi[:, c, :],
                                        ALU.subtract).then_inc(pT_lo_full, 1)

            def invert(tile, k):
                dve.wait_ge(pv_made, NB * tile + NB)
                if not (isinstance(tile, int) and tile < 2):
                    dve.wait_ge(gat_full, tile - 1)
                nc.vector.reciprocal(rden[:, k % 2:k % 2 + 1], out_ps[:, C:C + 1]).then_inc(rden_full, 1)

            def residual(tile, k, it):
                s = k % 2
                dve.wait_ge(gat_full, tile + 1)
                dve.wait_ge(x_res_full[k], 16 * it + 16)
                nc.vector.tensor_tensor(summed[:, s, :], gat[:, s, :], x_res[:, k, :],
                                        ALU.add).then_inc(summed_full, 1)
                dve.wait_ge(summed_full, tile + 1)
                nc.vector.bn_stats(stats[:, s, :], summed[:, s, :]).then_inc(stats_full, 1)
                dve.wait_ge(stats_full, 1)
                dve.wait_ge(stats_full, tile + 1)
                nc.vector.bn_aggr(meanvar[:, s, :], stats[:, s, :]).then_inc(meanvar_full, 1)
                dve.wait_ge(meanvar_full, tile + 1)
                nc.vector.tensor_scalar(vareps[:, s:s + 1], meanvar[:, s, 1:2], EPS, None,
                                        ALU.add).then_inc(vareps_full, 1)

            def normalise(tile, k, it):
                s = k % 2
                dve.wait_ge(rstd_full, tile + 1)
                if not (isinstance(it, int) and it == 0):
                    dve.wait_ge(x1_stored[k], 16 * it)
                nc.vector.tensor_scalar(x1_out[:, k, :], summed[:, s, :], meanvar[:, s, 0:1], rstd[:, s:s + 1],
                                        ALU.subtract, ALU.mult).then_inc(x1_full, 1)

            for k in range(TB):
                split_xT(k, k, 0, None)
                split_h3(k, k, 0)
            with dve.Fori(1, NB) as j:
                for k in range(TB):
                    split_xT(TB * j + k, k, j, None)
                    split_h3(TB * j + k, k, j)
            for k in range(TB):
                make_mask(k)
            split_y(0)
            mask(0, 0, 0)
            maximum(0, 0)

            def step(it, masks, preps, more):
                n = preps_before(it, preps)
                tile = TB * it
                for k in range(TB):
                    todo = list(PREP_AT[k]) if preps else []
                    made = sum(len(PREP_AT[i]) for i in range(k)) if preps else 0
                    if k > 0:
                        normalise(tile + k - 1, k - 1, it)
                    if todo:
                        split_xT(n + made, todo[0], prep_slot(it), NB * tile)

                    def first_splits(c, tile=tile, k=k):
                        split_pT(tile + k, c)

                    if k < TB - 1:
                        mask(tile + k + 1, k + 1, (it % NB) * TB + k + 1, first_splits)
                    elif more:
                        mask(tile + TB, 0, (it + 1) % NB * TB, first_splits)
                    else:
                        first_splits(0)
                        first_splits(1)
                    if k < TB - 1 or more:
                        maximum(tile + k + 1, k + 1)
                    if todo:
                        split_h3(n + made, todo[0], prep_slot(it))
                    for c in range(2, NB):
                        split_pT(tile + k, c)
                        if c == 2 and len(todo) > 1:
                            split_xT(n + made + 1, todo[1], prep_slot(it), NB * tile)
                    if NB == 2 and len(todo) > 1:
                        split_xT(n + made + 1, todo[1], prep_slot(it), NB * tile)
                    if len(todo) > 1:
                        split_h3(n + made + 1, todo[1], prep_slot(it))
                    if k == Y_SPLIT_AT and more:
                        split_y(it + 1)
                    if masks:
                        make_mask(TB * it + TB + k)
                    invert(tile + k, k)
                    residual(tile + k, k, it)
                normalise(tile + TB - 1, TB - 1, it)

            over_blocks(dve, step)

        @block.gpsimd
        def _(pool):
            with pool.Fori(0, BLOCKS) as it:
                for k in range(TB):
                    s = k % 2
                    pool.wait_ge(vareps_full, TB * it + k + 1)
                    nc.gpsimd.tensor_tensor(rstd[:, s:s + 1], vareps[:, s:s + 1], st.minus_half[:, 0:1],
                                            ALU.pow).then_inc(rstd_full, 1)


def build_edges(nc, st, W, a):
    NT, N = st.notadj.shape[1], st.notadj.shape[2]
    C = W.shape[0]
    KC = C // P
    D = a.shape[0] // 2
    H = C // D
    ident, notadj, adjT, edgeless, w_ext = st.ident, st.notadj, st.adjT, st.edgeless, st.w_ext
    with ExitStack() as ctx:
        def sb(name, shape, dt):
            return ctx.enter_context(nc.sbuf_tensor(name, shape, dt))

        def sem(name):
            return ctx.enter_context(nc.semaphore(name))

        edge_rows = sb("edge_rows", [P, 2, N], BF16)
        ident16 = sb("ident16", [P, P], BF16)
        ones16 = sb("ones16", [P, 2], BF16)
        a_rows = sb("a_rows", [P, 2, D], F32)
        w_in = sb("w_in", [P, KC, C], F32)
        products = sb("products", [P, KC, 3, C], F32)
        squares = sb("squares", [P, KC], F32)
        square_sum = sb("square_sum", [P, 3], F32)
        scale = sb("scale", [P, 2], F32)
        turned = ctx.enter_context(nc.psum_tensor("edges_turned_ps", [P, NT, P], BF16))
        degree = ctx.enter_context(nc.psum_tensor("degree", [P, N], F32))

        small_loaded = sem("small_loaded")
        rows_full = sem("rows_full")
        rows_turned = sem("rows_turned")
        rows_copied = sem("rows_copied")
        ident16_full = sem("ident16_full")
        degree_made = sem("degree_made")
        chain = sem("w_steps")
        squares_full = sem("squares_full")
        reduced = sem("reduced")
        scale_full = sem("scale_full")
        squares_ready = sem("squares_ready")
        scaled = sem("scaled")
        block = ctx.enter_context(nc.Block())

        @block.sync
        def _(sp):
            sp.dma_start(w_in[:], W.rearrange("(k p) d -> p k d", p=P)).then_inc(small_loaded, 16)
            sp.dma_start(a_rows[:].rearrange("p s d -> p (s d)"), a.partition_broadcast(P)).then_inc(small_loaded, 16)
            sp.wait_ge(small_loaded, 32)

        @block.gpsimd
        def _(pool):
            nc.gpsimd.memset(st.mean_ones[:], 1.0 / N)
            nc.gpsimd.memset(st.den_scale[:], DEN_SCALE)
            pool.wait_ge(squares_full, 1)
            nc.gpsimd.partition_all_reduce(square_sum[:, 1:2], square_sum[:, 0:1], P,
                                           bass.bass_isa.ReduceOp.add).then_inc(reduced, 1)
            pool.wait_ge(reduced, 1)
            nc.gpsimd.tensor_tensor(scale[:, 0:1], square_sum[:, 1:2], st.minus_half[:], ALU.pow).then_inc(scale_full, 1)

        @block.tensor
        def _(pe):
            pe.wait_ge(ident16_full, 1)
            with pe.Fori(0, NT // 2) as pair:
                for k in range(2):
                    pe.wait_ge(rows_full, 2 * pair + k + 1)
                    pe.wait_ge(rows_copied, 2 * pair + k)
                    for j in range(NT):
                        ins = nc.tensor.transpose(turned[:, j, :], edge_rows[:, k, j * P:(j + 1) * P], ident16[:])
                    ins.then_inc(rows_turned, 1)
            pe.wait_ge(rows_copied, NT)
            for j in range(NT):
                for c in range(N // CH):
                    ins = nc.tensor.matmul(degree[0:1, c * CH:(c + 1) * CH], ones16[:, 0:1],
                                           adjT[:, j, c * CH:(c + 1) * CH], start=(j == 0), stop=(j == NT - 1))
            ins.then_inc(degree_made, 1)

        @block.scalar
        def _(act):
            with act.Fori(0, NT) as t:
                act.wait_ge(rows_turned, t + 1)
                nc.scalar.activation(adjT[:, :, dynamic(t * P, P)], turned[:], ACT.Copy).then_inc(rows_copied, 1)

        @block.vector
        def _(dve):
            nc.vector.memset(ones16[:], 1.0)
            nc.vector.memset(st.mean_lo[:], 0.0)
            nc.vector.memset(st.mean_hi[:], DEN_SCALE)
            nc.vector.tensor_copy(ident16[:], ident[:]).then_inc(ident16_full, 1)
            with dve.Fori(0, NT // 2) as pair:
                for k in range(2):
                    dve.wait_ge(rows_turned, 2 * pair)
                    nc.vector.tensor_scalar(edge_rows[:, k, :],
                                            notadj[:, dynamic(2 * pair + k, 1), :].rearrange("p o n -> p (o n)"),
                                            -1.0, 1.0, ALU.mult, ALU.add).then_inc(rows_full, 1)
            dve.wait_ge(small_loaded, 32)
            for c in range(KC):
                for s in range(2):
                    for h in range(H):
                        cols = slice(h * D, (h + 1) * D)
                        nc.vector.tensor_tensor_reduce(
                            out=products[:, c, s, cols], in0=w_in[:, c, cols], in1=a_rows[:, s, :], scale=1.0,
                            scalar=0.0, op0=ALU.mult, op1=ALU.add,
                            accum_out=w_ext[:, c, C + s * H + h:C + s * H + h + 1]).then_inc(chain, 1)
                dve.wait_ge(chain, (c + 1) * 2 * H)
                nc.vector.tensor_tensor_reduce(
                    out=products[:, c, 2, :], in0=w_in[:, c, :], in1=w_in[:, c, :], scale=1.0,
                    scalar=1e-30, op0=ALU.mult, op1=ALU.add, accum_out=squares[:, c:c + 1]).then_inc(squares_ready, 1)
            dve.wait_ge(squares_ready, KC)
            nc.vector.tensor_reduce(square_sum[:, 0:1], squares[:], AX.X, ALU.add).then_inc(squares_full, 1)
            dve.wait_ge(scale_full, 1)
            nc.vector.tensor_scalar(scale[:, 1:2], scale[:, 0:1], Q_SCALE, None, ALU.mult).then_inc(scaled, 1)
            dve.wait_ge(scaled, 1)
            for c in range(KC):
                nc.vector.tensor_scalar(w_ext[:, c, 0:C], w_in[:, c, :], scale[:, 1:2], None, ALU.mult)
            nc.vector.reciprocal(square_sum[:, 2:3], scale[:, 1:2]).then_inc(scaled, 1)
            dve.wait_ge(scaled, 2)
            nc.vector.tensor_scalar(st.unscale[:], square_sum[:, 2:3], DEN_SCALE, None, ALU.mult)
            dve.wait_ge(degree_made, 1)
            nc.vector.tensor_scalar(edgeless[:], degree[0:1, :], 0.0, None, ALU.is_equal)


def build_heads(nc, st, x1, s_rows, out):
    B, N, C = x1.shape
    NT = N // P
    KC = C // P
    D = 64
    H = C // D
    E = D + 1
    Q = C + 2 * H
    GROUPS = CH // (2 * E)
    BANKS = -(-NT // GROUPS)
    DEPTH = 4
    RUNS = NT // DEPTH
    MID = RUNS // 2
    PAIRS = NT // 2
    PREP_HEADS = PAIRS // RUNS
    x1_rows = x1.rearrange("b n c -> (b n) c")
    out_rows = out.rearrange("b n c -> (b n) c")
    ident, adjT, edgeless, w_ext = st.ident, st.adjT, st.edgeless, st.w_ext
    mean_hi, mean_lo = st.mean_hi, st.mean_lo

    with ExitStack() as ctx:
        def sb(name, shape, dt):
            return ctx.enter_context(nc.sbuf_tensor(name, shape, dt))

        def sem(name):
            return ctx.enter_context(nc.semaphore(name))

        def ps(name, shape):
            return ctx.enter_context(nc.psum_tensor(name, shape, F32))

        x_in = sb("hx_in", [P, 2, C], F32)
        xT = sb("hxT", [P, 2, KC, P], F32)
        q = sb("q", [P, 2 * NT, Q], F32)
        s_cols = sb("s_cols", [P, H, NT], F32)
        s_turned_sb = sb("s_turned_sb", [H * NT, P], F32)
        s_all = sb("s_all", [P, 2, N], F32)
        d_max = sb("d_max", [P, 2, H], F32)
        d_less = sb("d_less", [P, NT, H], F32)
        s_more = sb("s_more", [P, NT, H], F32)
        d_huge = sb("d_huge", [P, 2 * NT, H], F32)
        low_factor = sb("low_factor", [P, 2 * NT, H], F32)
        up_factor = sb("up_factor", [P, 2 * NT, H], F32)
        row_factor = sb("row_factor", [P, 2 * NT, H], F32)
        values = sb("values", [P, 2, NT, E], F32)
        up_hi = sb("up_hi", [P, 2, NT, E], F16)
        up_lo = sb("up_lo", [P, 2, NT, E], F16)
        low_hi = sb("low_hi", [P, 2, NT, E], F16)
        low_lo = sb("low_lo", [P, 2, NT, E], F16)
        upper = sb("upper", [P, DEPTH, N], BF16)
        lower = sb("lower", [P, 2, N], BF16)
        acc_sb = sb("acc_sb", [P, NT, 2 * E], F32)
        rden = sb("hrden", [P, 2, NT], F32)
        h_out = sb("h_out", [P, NT, C], F32)
        x_res = sb("hx_res", [P, NT, D], F32)
        stats = sb("hstats", [P, NT, 6], F32)
        meanvar = sb("hmeanvar", [P, NT, 2], F32)
        vareps = sb("hvareps", [P, NT], F32)
        rstd = sb("hrstd", [P, NT], F32)
        pause = sb("pause", [P, 2], F32)

        weighted = acc_sb[:, :, 0:E]
        negative = acc_sb[:, :, E:E + D]

        acc = ps("acc", [P, BANKS, CH])
        turn_ps = ps("turn_ps", [P, CH])
        q_ps = ps("q_ps", [P, CH])

        x_in_full = [sem(f"hx_in_full{m}") for m in range(2)]
        x_turned = sem("hx_turned")
        xT_full = sem("hxT_full")
        q_made = sem("q_made")
        q_full = sem("q_full")
        s_cols_full = sem("s_cols_full")
        s_turned = sem("s_turned")
        s_turned_full = sem("s_turned_full")
        s_stored = sem("s_stored")
        s_all_full = [sem(f"s_all_full{k}") for k in range(2)]
        s_all_free = sem("s_all_free")
        d_max_part = sem("d_max_part")
        d_max_full = sem("d_max_full")
        differences_full = sem("differences_full")
        d_huge_full = sem("d_huge_full")
        factors_full = sem("factors_full")
        s_sum_full = sem("s_sum_full")
        mean_made = sem("mean_made")
        mean_hi_full = sem("mean_hi_full")
        mean_full = sem("mean_full")
        values_full = sem("values_full")
        v_hi_full = sem("v_hi_full")
        v_lo_full = sem("v_lo_full")
        step_full = sem("step_full")
        upper_full = sem("upper_full")
        lower_full = sem("lower_full")
        edges_free = sem("edges_free")
        acc_made = sem("acc_made")
        acc_read = sem("acc_read")
        acc_scaled = sem("acc_scaled")
        weighted_full = sem("weighted_full")
        rden_full = sem("hrden_full")
        mixed_full = sem("mixed_full")
        negative_full = sem("negative_full")
        exp_full = sem("exp_full")
        elu_full = sem("elu_full")
        x_res_full = sem("hx_res_full")
        summed_full = sem("hsummed_full")
        stats_full = sem("hstats_full")
        meanvar_full = sem("hmeanvar_full")
        vareps_full = sem("hvareps_full")
        rstd_full = sem("hrstd_full")
        out_full = sem("out_full")
        out_stored = sem("out_stored")

        block = ctx.enter_context(nc.Block())

        def over_batches(engine, step):
            step(0, False, True)
            if B > 2:
                with engine.Fori(1, B - 1) as b:
                    step(b, True, True)
            step(B - 1, True, False)

        def group(tile):
            return tile // GROUPS, tile % GROUPS * 2 * E

        def slot(b):
            return b % 2 * NT

        def of_batch(tensor, b):
            return tensor[:, dynamic(slot(b), NT), :] if not isinstance(b, int) else \
                tensor[:, slot(b):slot(b) + NT, :]

        def one(tensor, index):
            return tensor[:, dynamic(index, 1), :].rearrange("p o c -> p (o c)") if not isinstance(index, int) \
                else tensor[:, index, :]

        @block.sync
        def _(sp):
            def load_x(b, pair):
                sp.wait_ge(x_turned, PAIRS * b + pair)
                for m in range(2):
                    sp.dma_start(x_in[:, m, :], x1_rows[dynamic((NT * b + 2 * pair + m) * P, P), :]
                                 ).then_inc(x_in_full[m], 16)

            def store_s(b):
                sp.wait_ge(s_turned_full, b + 1)
                sp.dma_start(s_rows[dynamic(b, 1), :, :].rearrange("o r n -> (o r) n"), s_turned_sb[:]).then_inc(s_stored, 16)
                sp.wait_ge(s_stored, 16 * b + 16)

            def load_s(b, h):
                sp.wait_ge(s_all_free, H * b + h + 1)
                row = s_rows[dynamic(b, 1), h * NT:(h + 1) * NT, :].rearrange("o r n -> (o r n)")
                sp.dma_start(s_all[:, h % 2, :], row.partition_broadcast(P)).then_inc(s_all_full[h % 2], 16)

            with sp.Fori(0, PAIRS) as pair:
                load_x(0, pair)
            store_s(0)
            load_s(0, 0)
            load_s(0, 1)

            def step(b, before, prep):
                for h in range(H):
                    if prep and h < PREP_HEADS:
                        with sp.Fori(h * RUNS, (h + 1) * RUNS) as pair:
                            load_x(b + 1, pair)
                    if h + 2 < H:
                        load_s(b, h + 2)
                    elif prep:
                        if h + 2 == H:
                            store_s(b + 1)
                        load_s(b + 1, h + 2 - H)

            over_batches(sp, step)

        @block.tensor
        def _(pe):
            def turn(b, pair):
                for m in range(2):
                    pe.wait_ge(x_in_full[m], 16 * (PAIRS * b + pair) + 16)
                pe.wait_ge(xT_full, PAIRS * b + pair)
                if not (isinstance(b, int) and b == 0):
                    pe.wait_ge(s_turned_full, b)
                for m in range(2):
                    for c in range(KC):
                        ins = nc.tensor.transpose(turn_ps[:, (m * KC + c) * P:(m * KC + c + 1) * P],
                                                  x_in[:, m, c * P:(c + 1) * P], ident[:])
                ins.then_inc(x_turned, 1)

            def make_q(b, pair, m):
                pe.wait_ge(xT_full, PAIRS * b + pair + 1)
                pe.wait_ge(q_full, NT * b + 2 * pair + m)
                if not (isinstance(b, int) and b == 0):
                    pe.wait_ge(mean_full, b)
                for c in range(KC):
                    ins = nc.tensor.matmul(q_ps[:, 0:Q], xT[:, m, c, :], w_ext[:, c, :],
                                           start=(c == 0), stop=(c == KC - 1))
                ins.then_inc(q_made, 1)

            def s_and_mean(b):
                pe.wait_ge(s_cols_full, b + 1)
                pe.wait_ge(xT_full, PAIRS * b + PAIRS)
                pe.wait_ge(q_full, NT * b + NT)
                for t in range(NT):
                    ins = nc.tensor.matmul(q_ps[0:1, 0:C], st.mean_ones[:, 0:1], one(q, slot(b) + t)[:, 0:C],
                                           start=(t == 0), stop=(t == NT - 1))
                    if t == 0:
                        nc.tensor.transpose(turn_ps[0:H * NT, 0:P], s_cols[:].rearrange("p h t -> p (h t)"),
                                            ident[:]).then_inc(s_turned, 1)
                ins.then_inc(mean_made, 1)

            def products(b, h, run, prep):
                preparing = prep and h < PREP_HEADS
                if preparing:
                    turn(b + 1, RUNS * h + run)
                for k in range(DEPTH):
                    j = DEPTH * run + k
                    jn = (H * b + h) * NT + j
                    pe.wait_ge(lower_full, jn + 1)
                    for tile in range(NT):
                        bank, at = group(tile)
                        for edges, col, parts in ((upper[:, k, :], at, (up_hi, up_lo)),
                                                  (lower[:, k % 2, :], at + E, (low_hi, low_lo))):
                            for v in parts:
                                ins = nc.tensor.matmul(
                                    acc[:, bank, col:col + E], edges[:, tile * P:(tile + 1) * P],
                                    one(v[:, h % 2, :, :], j), start=False, stop=True, skip_group_check=True)
                    ins.then_inc(edges_free, 1)
                    if preparing and k % 2 == 1:
                        make_q(b + 1, RUNS * h + run, k // 2)

            pe.sem_inc(acc_read, BANKS)
            pe.sem_inc(edges_free, DEPTH)
            with pe.Fori(0, PAIRS) as pair:
                turn(0, pair)
                make_q(0, pair, 0)
                make_q(0, pair, 1)
            s_and_mean(0)

            def step(b, before, prep):
                pe.wait_ge(mean_full, b + 1)
                for h in range(H):
                    n = H * b + h
                    pe.wait_ge(v_lo_full, 2 * n + 2)
                    for tile in range(NT):
                        bank, at = group(tile)
                        if at == 0:
                            pe.wait_ge(acc_read, BANKS * n + bank + 1)
                        for m, mean in enumerate((mean_hi, mean_lo)):
                            nc.tensor.matmul(acc[:, bank, at:at + E], edgeless[0:1, tile * P:(tile + 1) * P],
                                             mean[0:1, h, :], start=(at == 0 and m == 0), stop=True,
                                             skip_group_check=True)
                    with pe.Fori(0, MID) as run:
                        products(b, h, run, prep)
                    if prep and h == H - 2:
                        s_and_mean(b + 1)
                    with pe.Fori(MID, RUNS) as run:
                        products(b, h, run, prep)
                    pe.wait_ge(edges_free, DEPTH + n * NT + NT)
                    pe.nop().then_inc(acc_made, 1)

            over_batches(pe, step)

        @block.scalar
        def _(act):
            def copy_xT(b, pair):
                act.wait_ge(x_turned, PAIRS * b + pair + 1)
                act.wait_ge(q_made, NT * b + 2 * pair)
                nc.scalar.activation(xT[:].rearrange("p m c n -> p (m c n)"), turn_ps[:, 0:2 * C],
                                     ACT.Copy).then_inc(xT_full, 1)

            def copy_q(b, pair, m):
                act.wait_ge(x_turned, 1)
                act.wait_ge(q_made, NT * b + 2 * pair + m + 1)
                if not (isinstance(b, int) and b == 0):
                    act.wait_ge(values_full, 2 * H * (b - 1))
                nc.scalar.activation(one(q, slot(b) + 2 * pair + m), q_ps[:, 0:Q], ACT.Copy).then_inc(q_full, 1)

            def copy_s(b):
                act.wait_ge(s_turned, b + 1)
                act.wait_ge(s_stored, 16 * b)
                nc.scalar.activation(s_turned_sb[:], turn_ps[0:H * NT, 0:P], ACT.Copy).then_inc(s_turned_full, 1)

            def factors(b):
                for tensor, source, scale in ((up_factor, d_less, 1.0), (low_factor, d_less, ALPHA),
                                              (row_factor, s_more, ALPHA - 1)):
                    act.wait_ge(d_huge_full, 1)
                    act.wait_ge(differences_full, 2 * b + 2)
                    if not (isinstance(b, int) and b == 0):
                        act.wait_ge(weighted_full, H * (b - 1))
                    nc.scalar.activation(of_batch(tensor, b), source[:], ACT.Exp, scale=scale).then_inc(factors_full, 1)
                act.wait_ge(mean_made, b + 1)
                if not (isinstance(b, int) and b == 0):
                    act.wait_ge(edges_free, (H * b - 1) * NT + DEPTH + 1)
                nc.scalar.activation(mean_hi[0:1, :, 0:D], q_ps[0:1, 0:C].rearrange("p (h d) -> p h d", h=H),
                                     ACT.Copy).then_inc(mean_hi_full, 1)

            def steps(b, h, run, tiles=range(DEPTH)):
                for k in tiles:
                    j = DEPTH * run + k
                    jn = (H * b + h) * NT + j
                    act.wait_ge(d_huge_full, 1)
                    act.wait_ge(edges_free, jn + 1)
                    nc.scalar.activation(upper[:, k, :], s_all[:, h % 2, :], ACT.Relu,
                                         bias=one(d_huge, slot(b) + j)[:, h:h + 1],
                                         scale=HUGE).then_inc(step_full, 1)

            def steps_and_q(b, h, run, prep, inside=None):
                pair = RUNS * h + run
                copies = prep and not (isinstance(pair, int) and not 0 < pair <= PAIRS) and h <= PREP_HEADS
                steps(b, h, run, (0, 1))
                if copies:
                    copy_q(b + 1, pair - 1, 0)
                steps(b, h, run, (2,))
                if inside:
                    inside()
                steps(b, h, run, (3,))
                if copies:
                    copy_q(b + 1, pair - 1, 1)
                if prep and h < PREP_HEADS:
                    copy_xT(b + 1, pair)

            def split_values(n, h, used):
                for m, hi in enumerate((up_hi, low_hi)):
                    act.wait_ge(values_full, 2 * n + m + 1)
                    if used is not None:
                        act.wait_ge(acc_made, used)
                    nc.scalar.activation(hi[:, h % 2, :, :], values[:, m, :, :], ACT.Copy).then_inc(v_hi_full, 1)

            def copy_acc(n):
                act.wait_ge(acc_made, n + 1)
                act.wait_ge(elu_full, n)
                for bank in range(BANKS):
                    tiles = min(GROUPS, NT - GROUPS * bank)
                    nc.scalar.activation(acc_sb[:, GROUPS * bank:GROUPS * bank + tiles, :].rearrange("p t e -> p (t e)"),
                                         acc[:, bank, 0:tiles * 2 * E], ACT.Copy).then_inc(acc_read, 1)

            def elu_exp(n):
                act.wait_ge(negative_full, n + 1)
                nc.scalar.activation(negative, negative, ACT.Exp).then_inc(exp_full, 1)

            act.sem_inc(s_all_free, 2)
            with act.Fori(0, PAIRS) as pair:
                copy_xT(0, pair)
                copy_q(0, pair, 0)
                copy_q(0, pair, 1)
            copy_s(0)
            factors(0)
            split_values(0, 0, None)

            def step(b, before, prep):
                act.wait_ge(d_huge_full, b + 1)
                for h in range(H):
                    n = H * b + h
                    follows = before or h > 0
                    act.wait_ge(s_all_full[h % 2], 16 * (H // 2 * b + h // 2) + 16)
                    steps_and_q(b, h, 0, prep, (lambda m=n - 1: copy_acc(m)) if follows else None)
                    still = prep and h < PREP_HEADS
                    if MID > 1:
                        with act.Fori(1, MID) as run:
                            steps_and_q(b, h, run, still)
                    if h + 1 < H:
                        split_values(n + 1, h + 1, H * b + h if h > 0 or before else None)
                    if prep and h == H - 1:
                        factors(b + 1)
                    if MID < RUNS - 1:
                        with act.Fori(MID, RUNS - 1) as run:
                            steps_and_q(b, h, run, still)
                    if follows:
                        elu_exp(n - 1)
                    steps_and_q(b, h, RUNS - 1, still)
                    if prep and h == H - 2:
                        copy_s(b + 1)
                    if prep and h == H - 1:
                        split_values(H * b + H, 0, H * b + H - 1)
                    act.wait_ge(step_full, n * NT + NT)
                    act.sem_inc(s_all_free, 1)

            over_batches(act, step)
            copy_acc(H * B - 1)
            elu_exp(H * B - 1)

        @block.gpsimd
        def _(pool):
            def top_of_d(b):
                pool.wait_ge(d_max_part, b + 1)
                nc.gpsimd.tensor_tensor(pause[:, 0:1], st.minus_half[:], st.minus_half[:], ALU.add)
                nc.gpsimd.partition_all_reduce(d_max[:, 1, :], d_max[:, 0, :], P,
                                               bass.bass_isa.ReduceOp.max).then_inc(d_max_full, 1)

            def make_values(b, h):
                for m, factor in enumerate((up_factor, low_factor)):
                    pool.wait_ge(factors_full, 1)
                    pool.wait_ge(factors_full, 3 * b + 2)
                    pool.wait_ge(v_lo_full, 2 * (H * b + h))
                    own = of_batch(factor, b)[:, :, h:h + 1]
                    nc.gpsimd.tensor_tensor(values[:, m, :, 0:D], of_batch(q, b)[:, :, h * D:(h + 1) * D],
                                            own.to_broadcast([P, NT, D]), ALU.mult)
                    nc.gpsimd.tensor_tensor(values[:, m, :, D:E], own,
                                            st.den_scale[:, 0:1].unsqueeze(1).to_broadcast([P, NT, 1]),
                                            ALU.mult).then_inc(values_full, 1)

            def split_values(b, h):
                for m, (hi, lo) in enumerate(((up_hi, up_lo), (low_hi, low_lo))):
                    pool.wait_ge(v_hi_full, 2 * (H * b + h) + m + 1)
                    nc.gpsimd.tensor_tensor(lo[:, h % 2, :, :], values[:, m, :, :], hi[:, h % 2, :, :],
                                            ALU.subtract).then_inc(v_lo_full, 1)

            def add_parts(b, h):
                n = H * b + h
                pool.wait_ge(factors_full, 1)
                pool.wait_ge(acc_read, BANKS * (n + 2))
                nc.gpsimd.tensor_tensor(acc_sb[:, :, E:2 * E], acc_sb[:, :, E:2 * E],
                                        of_batch(row_factor, b)[:, :, h:h + 1].to_broadcast([P, NT, E]),
                                        ALU.mult).then_inc(acc_scaled, 1)
                pool.wait_ge(acc_scaled, n + 1)
                nc.gpsimd.tensor_tensor(weighted, acc_sb[:, :, 0:E], acc_sb[:, :, E:2 * E],
                                        ALU.add).then_inc(weighted_full, 1)

            def load_residual(b, h):
                pool.wait_ge(summed_full, H * b + h)
                rows = x1_rows[dynamic(N * b, N), h * D:(h + 1) * D].rearrange("(t p) d -> p t d", p=P)
                pool.dma_start(x_res[:], rows).then_inc(x_res_full, 16)

            def invert_deviation(b):
                pool.wait_ge(vareps_full, b + 1)
                nc.gpsimd.tensor_tensor(rstd[:], vareps[:], st.minus_half[:, 0:1].to_broadcast([P, NT]),
                                        ALU.pow).then_inc(rstd_full, 1)

            def store(b):
                for half in range(2):
                    pool.wait_ge(out_full, 2 * b + half + 1)
                    pool.dma_start(out_rows[dynamic(N * b + half * N // 2, N // 2), :].rearrange("(t p) c -> p t c", p=P),
                                   h_out[:, half * NT // 2:(half + 1) * NT // 2, :]).then_inc(out_stored, 16)

            top_of_d(0)
            make_values(0, 0)
            split_values(0, 0)

            def step(b, before, prep):
                for h in range(H):
                    if h + 1 < H:
                        make_values(b, h + 1)
                    if h > 0:
                        load_residual(b, h - 1)
                        add_parts(b, h - 1)
                    elif before:
                        load_residual(b - 1, H - 1)
                        add_parts(b - 1, H - 1)
                    if before and h == 1:
                        store(b - 1)
                    if h + 1 < H:
                        split_values(b, h + 1)
                    if before and h == 0:
                        invert_deviation(b - 1)
                    if prep and h == H - 2:
                        top_of_d(b + 1)
                    if prep and h == H - 1:
                        make_values(b + 1, 0)
                        split_values(b + 1, 0)

            over_batches(pool, step)
            load_residual(B - 1, H - 1)
            add_parts(B - 1, H - 1)
            invert_deviation(B - 1)
            store(B - 1)
            pool.wait_ge(out_stored, 32 * B)

        @block.vector
        def _(dve):
            def s_and_top(b):
                d = of_batch(q, b)[:, :, C + H:Q]
                dve.wait_ge(q_full, 1)
                dve.wait_ge(q_full, NT * b + NT)
                dve.wait_ge(s_turned, b)
                nc.vector.tensor_copy(s_cols[:], of_batch(q, b)[:, :, C:C + H].rearrange("p t h -> p h t")).then_inc(s_cols_full, 1)
                nc.vector.tensor_reduce(d_max[:, 0, :], d.rearrange("p t h -> p h t"), AX.X,
                                        ALU.max).then_inc(d_max_part, 1)
                if not (isinstance(b, int) and b == 0):
                    dve.wait_ge(q_full, 1)
                    dve.wait_ge(step_full, H * NT * (b - 1))
                nc.vector.tensor_scalar(of_batch(d_huge, b), d, HUGE, None, ALU.mult).then_inc(d_huge_full, 1)

            def differences(b):
                dve.wait_ge(q_full, 1)
                dve.wait_ge(d_max_full, b + 1)
                dve.wait_ge(factors_full, 3 * b)
                top = d_max[:, 1, :].unsqueeze(1).to_broadcast([P, NT, H])
                nc.vector.tensor_tensor(d_less[:], of_batch(q, b)[:, :, C + H:Q], top, ALU.subtract).then_inc(differences_full, 1)
                nc.vector.tensor_tensor(s_more[:], of_batch(q, b)[:, :, C:C + H], top, ALU.add).then_inc(s_sum_full, 1)
                dve.wait_ge(s_sum_full, b + 1)
                nc.vector.tensor_scalar(s_more[:], s_more[:], 0.0, None, ALU.max).then_inc(differences_full, 1)

            def split_mean(b):
                dve.wait_ge(mean_hi_full, b + 1)
                nc.vector.tensor_tensor(mean_lo[0:1, :, 0:D], q_ps[0:1, 0:C].rearrange("p (h d) -> p h d", h=H),
                                        mean_hi[0:1, :, 0:D], ALU.subtract).then_inc(mean_full, 1)

            def edges(b, h, run, inside=None):
                for two in range(0, DEPTH, 2):
                    tiles = []
                    for k in (two, two + 1):
                        j = DEPTH * run + k
                        jn = (H * b + h) * NT + j
                        adjacent = one(adjT, j)
                        tiles.append((k, jn, adjacent))
                        dve.wait_ge(step_full, jn + 1)
                        nc.vector.tensor_tensor(upper[:, k, :], upper[:, k, :], adjacent,
                                                ALU.min).then_inc(upper_full, 1)
                    for k, jn, adjacent in tiles:
                        dve.wait_ge(upper_full, jn + 1)
                        dve.wait_ge(edges_free, jn + (DEPTH - 1))
                        nc.vector.tensor_tensor(lower[:, k % 2, :], adjacent, upper[:, k, :],
                                                ALU.subtract).then_inc(lower_full, 1)
                    if inside and two == 0:
                        inside()

            def mix(b, h):
                n = H * b + h
                dve.wait_ge(weighted_full, n + 1)
                nc.vector.reciprocal(rden[:, 0, :], weighted[:, :, D:E].rearrange("p t o -> p (t o)")).then_inc(rden_full, 1)
                dve.wait_ge(rden_full, 2 * n + 1)
                nc.vector.tensor_scalar(rden[:, 1, :], rden[:, 0, :], st.unscale[:, 0:1], None, ALU.mult).then_inc(rden_full, 1)
                dve.wait_ge(rden_full, 2 * n + 2)
                dve.wait_ge(out_stored, 32 * b)
                nc.vector.tensor_tensor(h_out[:, :, h * D:(h + 1) * D], weighted[:, :, 0:D],
                                        rden[:, 1, :].unsqueeze(2).to_broadcast([P, NT, D]),
                                        ALU.mult).then_inc(mixed_full, 1)
                dve.wait_ge(mixed_full, n + 1)
                nc.vector.tensor_scalar(negative, h_out[:, :, h * D:(h + 1) * D], 0.0, None,
                                        ALU.min).then_inc(negative_full, 1)

            def elu(b, h):
                n = H * b + h
                own = h_out[:, :, h * D:(h + 1) * D]
                dve.wait_ge(exp_full, n + 1)
                nc.vector.scalar_tensor_tensor(out=own, in0=own, scalar=0.0, in1=negative, op0=ALU.max,
                                               op1=ALU.add).then_inc(elu_full, 1)
                dve.wait_ge(elu_full, n + 1)
                dve.wait_ge(x_res_full, 16 * n + 16)
                nc.vector.scalar_tensor_tensor(out=own, in0=own, scalar=-1.0, in1=x_res[:], op0=ALU.add,
                                               op1=ALU.add).then_inc(summed_full, 1)

            def moments(b):
                dve.wait_ge(summed_full, H * (b + 1))
                for t in range(NT):
                    nc.vector.bn_stats(stats[:, t, :], h_out[:, t, :]).then_inc(stats_full, 1)
                dve.wait_ge(stats_full, NT * (b + 1))
                nc.vector.memset(pause[:, 1:2], 0.0)
                for t in range(NT):
                    nc.vector.bn_aggr(meanvar[:, t, :], stats[:, t, :]).then_inc(meanvar_full, 1)
                dve.wait_ge(meanvar_full, NT * (b + 1))
                nc.vector.tensor_scalar(vareps[:], meanvar[:, :, 1:2].rearrange("p t o -> p (t o)"), EPS, None,
                                        ALU.add).then_inc(vareps_full, 1)

            def normalise(b, half):
                dve.wait_ge(rstd_full, b + 1)
                for t in range(half * NT // 2, (half + 1) * NT // 2):
                    ins = nc.vector.tensor_scalar(h_out[:, t, :], h_out[:, t, :], meanvar[:, t, 0:1], rstd[:, t:t + 1],
                                                  ALU.subtract, ALU.mult)
                ins.then_inc(out_full, 1)

            s_and_top(0)
            differences(0)
            split_mean(0)

            def step(b, before, prep):
                for h in range(H):
                    finishing = before and h == 1
                    edges(b, h, 0, (lambda m=b - 1: normalise(m, 0)) if finishing else None)
                    if finishing:
                        normalise(b - 1, 1)
                    if prep and h == H - 2:
                        s_and_top(b + 1)
                    if MID > 1:
                        with dve.Fori(1, MID) as run:
                            edges(b, h, run)
                    if h > 0:
                        mix(b, h - 1)
                    elif before:
                        mix(b - 1, H - 1)
                    with dve.Fori(MID, RUNS) as run:
                        edges(b, h, run)
                    if h > 0:
                        elu(b, h - 1)
                    elif before:
                        elu(b - 1, H - 1)
                    if before and h == 0:
                        moments(b - 1)
                    if prep and h == H - 2:
                        differences(b + 1)
                    if prep and h == H - 1:
                        split_mean(b + 1)

            over_batches(dve, step)
            mix(B - 1, H - 1)
            elu(B - 1, H - 1)
            moments(B - 1)
            normalise(B - 1, 0)
            normalise(B - 1, 1)
class Store:
    pass


def bass_two_graph_layers(nc, x, adj, W1, W2, W3, W, a, out):
    B, N, C = x.shape
    x1 = nc.dram_tensor("x1", x.shape, F32, kind="Internal").ap()
    s_rows = nc.dram_tensor("s_rows", (B, N // P * (C // (a.shape[0] // 2)), P), F32, kind="Internal").ap()
    st = Store()
    with ExitStack() as ctx:
        def sb(name, shape, dt):
            return ctx.enter_context(nc.sbuf_tensor(name, shape, dt))

        st.ident = sb("ident", [P, P], F32)
        st.minus_half = sb("minus_half", [P, 1], F32)
        mask = ctx.enter_context(ExitStack())
        st.notadj = mask.enter_context(nc.sbuf_tensor("notadj", [P, N // P, N], U8, side="right"))
        with ExitStack() as dense:
            def sd(name, shape, dt):
                return dense.enter_context(nc.sbuf_tensor(name, shape, dt))
            st.w3 = sd("w3", [P, 2, C], F32)
            st.a_hi = sd("a_hi", [P, 2, C], F32R)
            st.a_lo = sd("a_lo", [P, 2, C], F32R)
            st.h3_hi = sd("h3_hi", [P, 2 * (N // P), C + 1], F16)
            build_setup(nc, st, W1, W2, W3)
            build_dense(nc, st, x, adj, x1)
        NT = N // P
        H = C // (a.shape[0] // 2)
        E = C // H + 1
        st.adjT = sb("adjT", [P, NT, N], BF16)
        st.edgeless = sb("edgeless", [1, N], BF16)
        st.w_ext = sb("w_ext", [P, C // P, C + 2 * H], F32)
        st.unscale = sb("unscale", [P, 1], F32)
        st.den_scale = sb("den_scale", [P, 1], F32)
        st.mean_ones = sb("mean_ones", [P, 1], F32)
        st.mean_hi = sb("mean_hi", [1, H, E], F16)
        st.mean_lo = sb("mean_lo", [1, H, E], F16)
        build_edges(nc, st, W, a)
        mask.close()
        build_heads(nc, st, x1, s_rows, out)


_INS = ["x", "adj", "L0_gnn_W1", "L0_gnn_W2", "L0_gnn_W3", "L1_gnn_W", "L1_gnn_a"]


def kernel(**inputs):
    import numpy as _np
    import concourse.bacc as _bacc
    from concourse import mybir as _mybir
    from concourse.bass_utils import run_bass_kernel_spmd as _run

    nc = _bacc.Bacc("TRN2", target_bir_lowering=False, num_devices=1)
    arrays, args = {}, []
    for name in _INS:
        a = _np.ascontiguousarray(inputs[name])
        arrays[f"in_{name}_dram"] = a
        args.append(nc.dram_tensor(f"in_{name}_dram", a.shape, _mybir.dt.from_np(a.dtype), kind="ExternalInput").ap())
    shape = inputs["x"].shape
    args.append(nc.dram_tensor("out_0_dram", shape, _mybir.dt.float32, kind="ExternalOutput").ap())
    bass_two_graph_layers(nc, *args)
    r = _run(nc, [arrays], core_ids=[0])
    return r.results[0]["out_0_dram"]
```
